# Optimizing a Trainium2 kernel written in Bass

```python
import numpy as np
import jax
import jax.numpy as jnp

def _softmax(x, axis=-1):
    return jax.nn.softmax(x, axis=axis)

def _gelu(x):
    return jax.nn.gelu(x, approximate=True)

def _silu(x):
    return jax.nn.silu(x)

def _sigmoid(x):
    return jax.nn.sigmoid(x)

def _layernorm(x, axis=-1, eps=1e-05):
    m = jnp.mean(x, axis=axis, keepdims=True)
    v = jnp.var(x, axis=axis, keepdims=True)
    return (x - m) / jnp.sqrt(v + eps)

def _scatter_add(tgt, idx, src, axis=0):
    return tgt.at[idx].add(src)

def _segment_sum(src, seg, n):
    return jax.ops.segment_sum(src, seg, n)
kernel_name = 'mk_macaron_d1_jaxref_r8_0481f6'

def setup_inputs(seed: int=0):
    np.random.seed(seed)
    _w = jnp.asarray

    def _L0_attn_setup():
        import jax, jax.numpy as jnp
        import numpy as np
        key = jax.random.key(seed)
        ks = jax.random.split(key, 6)
        B_, S, D, N = (8, 512, 128, 16)
        return {'x': jax.random.normal(ks[0], (B_, S, D), dtype=jnp.float32), 'A': jax.random.normal(ks[1], (N, N), dtype=jnp.float32), 'B': jax.random.normal(ks[2], (D, N), dtype=jnp.float32), 'C': jax.random.normal(ks[3], (N, D), dtype=jnp.float32), 'W_out': jax.random.normal(ks[4], (D, D), dtype=jnp.float32) * 0.02, 'b_out': jax.random.normal(ks[5], (D,), dtype=jnp.float32) * 0.02}
    _L0_attn_in = _L0_attn_setup()

    def _L0_ffn_setup():
        import jax, jax.numpy as jnp
        import numpy as np
        D_IN, D_HID = (128, 512)

        def _ternary(key, shape):
            return jax.random.randint(key, shape, -1, 2).astype(jnp.float32)

        def _tlin(x, w, s):
            return jnp.einsum('bsi,oi->bso', x, w) * s
        key = jax.random.key(seed)
        ks = jax.random.split(key, 12)
        inv = lambda fan: 1.0 / np.sqrt(fan).astype(np.float32)
        return {'x': jax.random.normal(ks[0], (4, 256, D_IN), dtype=jnp.float32), 'w1_w': _ternary(ks[1], (D_HID, D_IN)), 'w1_s': jax.random.uniform(ks[2], (D_HID,), dtype=jnp.float32) * inv(D_IN), 'w2_w': _ternary(ks[3], (D_HID, D_IN)), 'w2_s': jax.random.uniform(ks[4], (D_HID,), dtype=jnp.float32) * inv(D_IN), 'h1_w': _ternary(ks[5], (D_HID, D_HID)), 'h1_s': jax.random.uniform(ks[6], (D_HID,), dtype=jnp.float32) * inv(D_HID), 'h2_w': _ternary(ks[7], (D_HID, D_HID)), 'h2_s': jax.random.uniform(ks[8], (D_HID,), dtype=jnp.float32) * inv(D_HID), 'w3_w': _ternary(ks[9], (D_IN, D_HID)), 'w3_s': jax.random.uniform(ks[10], (D_IN,), dtype=jnp.float32) * inv(D_HID)}
    _L0_ffn_in = _L0_ffn_setup()
    _d = {'L0_attn_x': _L0_attn_in['x'], 'L0_attn_A': _L0_attn_in['A'], 'L0_attn_B': _L0_attn_in['B'], 'L0_attn_C': _L0_attn_in['C'], 'L0_attn_W_out': _L0_attn_in['W_out'], 'L0_attn_b_out': _L0_attn_in['b_out'], 'L0_ffn_w1_w': _L0_ffn_in['w1_w'], 'L0_ffn_w1_s': _L0_ffn_in['w1_s'], 'L0_ffn_w2_w': _L0_ffn_in['w2_w'], 'L0_ffn_w2_s': _L0_ffn_in['w2_s'], 'L0_ffn_h1_w': _L0_ffn_in['h1_w'], 'L0_ffn_h1_s': _L0_ffn_in['h1_s'], 'L0_ffn_h2_w': _L0_ffn_in['h2_w'], 'L0_ffn_h2_s': _L0_ffn_in['h2_s'], 'L0_ffn_w3_w': _L0_ffn_in['w3_w'], 'L0_ffn_w3_s': _L0_ffn_in['w3_s']}
    _x0 = _d['L0_attn_x']
    _d['L0_attn_x'] = jax.random.normal(jax.random.fold_in(jax.random.key(seed), 1), (8, 512, 128), dtype=_x0.dtype)
    del _x0
    return _d

def reference(L0_attn_x, L0_attn_A, L0_attn_B, L0_attn_C, L0_attn_W_out, L0_attn_b_out, L0_ffn_w1_w, L0_ffn_w1_s, L0_ffn_w2_w, L0_ffn_w2_s, L0_ffn_h1_w, L0_ffn_h1_s, L0_ffn_h2_w, L0_ffn_h2_s, L0_ffn_w3_w, L0_ffn_w3_s):

    def _L0_attn_ref(x, A, B, C, W_out, b_out):
        import jax, jax.numpy as jnp
        import numpy as np
        xB = jnp.einsum('bsd,dn->sbn', x, B)
        h0 = jnp.zeros((x.shape[0], A.shape[0]), dtype=x.dtype)

        def step(h, xb_t):
            h = jnp.tanh(xb_t + h @ A.T)
            return (h, h)
        _, hs = jax.lax.scan(step, h0, xB)
        y = jnp.einsum('sbn,nd->bsd', hs, C)
        return y @ W_out.T + b_out

    def _L0_ffn_ref(x, w1_w, w1_s, w2_w, w2_s, h1_w, h1_s, h2_w, h2_s, w3_w, w3_s):
        import jax, jax.numpy as jnp
        import numpy as np
        D_IN, D_HID = (128, 512)

        def _ternary(key, shape):
            return jax.random.randint(key, shape, -1, 2).astype(jnp.float32)

        def _tlin(x, w, s):
            return jnp.einsum('bsi,oi->bso', x, w) * s
        h = jax.nn.silu(_tlin(x, w1_w, w1_s)) * _tlin(x, w2_w, w2_s)
        h = jax.nn.gelu(_tlin(h, h1_w, h1_s), approximate=False)
        h = jax.nn.gelu(_tlin(h, h2_w, h2_s), approximate=False)
        return _tlin(h, w3_w, w3_s)
    x = L0_attn_x
    x = x + 0.5 * _L0_ffn_ref(_layernorm(x, axis=-1), L0_ffn_w1_w, L0_ffn_w1_s, L0_ffn_w2_w, L0_ffn_w2_s, L0_ffn_h1_w, L0_ffn_h1_s, L0_ffn_h2_w, L0_ffn_h2_s, L0_ffn_w3_w, L0_ffn_w3_s)
    x = x + _L0_attn_ref(_layernorm(x, axis=-1), L0_attn_A, L0_attn_B, L0_attn_C, L0_attn_W_out, L0_attn_b_out)
    x = x + 0.5 * _L0_ffn_ref(_layernorm(x, axis=-1), L0_ffn_w1_w, L0_ffn_w1_s, L0_ffn_w2_w, L0_ffn_w2_s, L0_ffn_h1_w, L0_ffn_h1_s, L0_ffn_h2_w, L0_ffn_h2_s, L0_ffn_w3_w, L0_ffn_w3_s)
    return x

_drawn_inputs = setup_inputs


def setup_inputs(seed=0):
    import zlib

    import numpy as np

    out = dict(_drawn_inputs(seed))
    spreads = {}
    factors = {}
    for name, (base, spread) in spreads.items():
        noise = np.random.default_rng([zlib.crc32(name.encode()), seed]).standard_normal(out[name].shape)
        drawn = base * np.exp(spread * noise) if base else spread * noise
        out[name] = jnp.asarray(drawn.astype(out[name].dtype))
    for name, factor in factors.items():
        out[name] = (out[name] * factor).astype(out[name].dtype)
    return out
```

```python
from contextlib import ExitStack

import concourse.bass as bass
from concourse import mybir

F32 = mybir.dt.float32
F32R = mybir.dt.float32r
I32 = mybir.dt.int32
ALU = mybir.AluOpType
ACT = mybir.ActivationFunctionType

P = 128
SEQS = 8
LENGTH = 512
STATES = 16
BLOCKS = 8
ROUNDS = BLOCKS - 1
STEPS = LENGTH // BLOCKS
CHUNKS = 8
CSTEPS = STEPS // CHUNKS
HCOLS = CSTEPS * BLOCKS
N = SEQS * HCOLS
HID = 512
KT = HID // P
QT = N // P
EPS = 1e-5


def wait(engine, sem, value):
    if isinstance(value, int) and value <= 0:
        return
    engine.wait_ge(sem, value)


def build(nc, xT, w1T, w2T, h1T, h2T, w3T, scales, AT, Bm, CTrep, WoutT, ident_d, mask_d, outT):
    with ExitStack() as ctx:
        def sb(name, shape, dt=F32):
            return ctx.enter_context(nc.sbuf_tensor(name, shape, dt))

        def bank(name):
            return ctx.enter_context(nc.psum_tensor(name, [P, N], F32))

        def sem(name):
            return ctx.enter_context(nc.semaphore(name))

        WCOLS = [HID, HID, KT * HID, KT * HID, KT * P]
        WOFF = [sum(WCOLS[:i]) for i in range(6)]
        w_raw = sb("w_raw", [P, WOFF[5]])
        w_hi = sb("w_hi", [P, WOFF[5]], F32R)
        w_lo = sb("w_lo", [P, WOFF[5]], F32R)
        ne_cnt = sb("ne_cnt", [P, 5])
        ne_sum = sb("ne_sum", [P, 1])
        sc = sb("sc", [P, 4 * KT + 2])
        s1h = sb("s1h", [P, KT])
        s12h = sb("s12h", [P, KT])
        s3h = sb("s3h", [P, 1])
        ident = sb("ident", [P, P])
        mask = sb("mask", [P, SEQS])
        ones = sb("ones", [P, 1])
        a_blk = sb("a_blk", [P, P])
        b_sb = sb("b_sb", [P, STATES])
        b_pad = sb("b_pad", [P, SEQS, P])
        ct = sb("ct", [P, P])
        wout = sb("wout", [P, P])
        cw = sb("cw", [P, P])
        cw_pad = sb("cw_pad", [P, SEQS, P])
        x_all = sb("x_all", [P, CHUNKS * N])
        x2_all = sb("x2_all", [P, CHUNKS * N])
        lnin = sb("lnin", [P, N])
        x1c = sb("x1c", [P, N])
        outb = sb("outb", [P, N])
        st_f = sb("st_f", [P, QT, 6])
        st_m = sb("st_m", [P, QT, 6])
        mv_f = sb("mv_f", [P, QT, 2])
        mv_m = sb("mv_m", [P, QT, 2])
        ve_f = sb("ve_f", [P, QT])
        ve_m = sb("ve_m", [P, QT])
        rs_f = sb("rs_f", [P, QT])
        rs_m = sb("rs_m", [P, QT])
        spare = sb("spare", [P, 1])
        mhalf = sb("mhalf", [P, QT])
        epsc = sb("epsc", [P, QT])
        xnt_f = sb("xnt_f", [P, N])
        xnt_m = sb("xnt_m", [P, N])
        xn_hi = sb("xn_hi", [P, N], F32R)
        xn_lo = sb("xn_lo", [P, N], F32R)
        xn2 = sb("xn2", [P, N])
        xb_all = sb("xb_all", [P, CHUNKS * HCOLS])
        h_all = sb("h_all", [P, BLOCKS + STEPS * BLOCKS])
        h_ne = sb("h_ne", [P, BLOCKS])
        h_nes = sb("h_nes", [P, 1])
        again = sb("again", [1, 1], I32)
        general = sb("general", [1, 1], I32)
        th = sb("th", [P, 2, N])
        u = sb("u", [P, 2, N])
        y1 = sb("y1", [P, KT, N])
        w_ne = y1[:, :, :].rearrange("p k n -> p (k n)")
        y23 = sb("y23", [P, KT, N])
        y1_hi = sb("y1_hi", [P, KT, N], F32R)
        y1_lo = sb("y1_lo", [P, KT, N], F32R)
        y2_hi = sb("y2_hi", [P, KT, N], F32R)
        y2_lo = sb("y2_lo", [P, KT, N], F32R)
        y3_hi = sb("y3_hi", [P, KT, N], F32R)
        y3_lo = sb("y3_lo", [P, KT, N], F32R)

        F = [bank(f"F{i}") for i in range(5)]
        FR = bank("FR")
        MI = bank("MI")
        SC = bank("SC")
        B2 = [F[0], F[1], F[2], F[3]]
        B1 = [(F[4], F[0]), (F[1], F[2]), (F[4], F[0]), (F[2], F[3])]
        B3 = [F[3], F[1], F[4], F[0]]
        B4 = F[1]

        ld_w = [sem(f"ld_w{i}") for i in range(5)]
        ld_sc = sem("ld_sc")
        ld_c = sem("ld_c")
        ld_a = sem("ld_a")
        ld_ab = sem("ld_ab")
        ld_x = sem("ld_x")
        ld_xall = sem("ld_xall")
        set_up = sem("set_up")
        pool_set = sem("pool_set")
        w_hi_ready = sem("w_hi_ready")
        w_lo_ready = sem("w_lo_ready")
        ne_ready = sem("ne_ready")
        gen_mm = sem("gen_mm")
        gen_ready = sem("gen_ready")
        cw_mm = sem("cw_mm")
        cw_ready = sem("cw_ready")
        tok = {k: sem(f"tok_{k}") for k in "fm"}
        bns = {k: sem(f"bns_{k}") for k in "fm"}
        var = {k: sem(f"var_{k}") for k in "fm"}
        veps = {k: sem(f"veps_{k}") for k in "fm"}
        rstd = {k: sem(f"rstd_{k}") for k in "fm"}
        normed = {k: sem(f"normed_{k}") for k in "fm"}
        feat = {k: sem(f"feat_{k}") for k in "fm"}
        xn_hi_r = sem("xn_hi_r")
        xn_lo_r = sem("xn_lo_r")
        l1_mm = sem("l1_mm")
        th_r = sem("th_r")
        u_r = sem("u_r")
        y1_r = sem("y1_r")
        y1_hi_r = sem("y1_hi_r")
        y1_lo_r = sem("y1_lo_r")
        l2_mm = sem("l2_mm")
        y2_hi_r = sem("y2_hi_r")
        y2_lo_dve = sem("y2_lo_dve")
        y2_lo_pool = sem("y2_lo_pool")
        l3_mm = sem("l3_mm")
        y3_hi_r = sem("y3_hi_r")
        y3_lo_dve = sem("y3_lo_dve")
        y3_lo_pool = sem("y3_lo_pool")
        l4_mm = sem("l4_mm")
        l4_out = sem("l4_out")
        x1_saved = sem("x1_saved")
        xn2_r = sem("xn2_r")
        xb_mm = sem("xb_mm")
        xb_r = sem("xb_r")
        step_mm = sem("step_mm")
        step_h = sem("step_h")
        ends_r = sem("ends_r")
        h_ne_r = sem("h_ne_r")
        h_nes_r = sem("h_nes_r")
        agree_mm = sem("agree_mm")
        again_r = sem("again_r")
        att_mm = sem("att_mm")
        x2_r = sem("x2_r")
        x2_saved = sem("x2_saved")
        out_sem = sem("out_sem")

        block = ctx.enter_context(nc.Block())

        def wtile(w, layer, k, m):
            width = P if layer == 4 else HID
            off = WOFF[layer] + k * width + m * P
            return w[:, off:off + P]

        def cols(t, c, width=N):
            return t[:, bass.ds(c * width, width)]

        FIRST_ROUND = CHUNKS

        @block.tensor
        def _(pe):
            def split_mm(out, layer, k, m, hi, lo, first, last, gen):
                pairs = [(w_hi, hi), (w_hi, lo)] + ([(w_lo, hi), (w_lo, lo)] if gen else [])
                for i, (w, y) in enumerate(pairs):
                    mm = nc.tensor.matmul(out, wtile(w, layer, k, m), y, start=first and i == 0,
                                          stop=last and i == len(pairs) - 1)
                return mm

            def to_tokens(kind, src, bankt, g, ready, value):
                pe.wait_ge(ready, value)
                if kind == "f":
                    wait(pe, xn_lo_r, g)
                else:
                    wait(pe, xb_r, g)
                for q in range(QT):
                    mm = nc.tensor.transpose(bankt[:, q * P:(q + 1) * P], src[:, q * P:(q + 1) * P], ident[:, :])
                mm.then_inc(tok[kind], 1)

            def to_features(kind, src, bankt, g):
                pe.wait_ge(normed[kind], g + 1)
                for q in range(QT):
                    mm = nc.tensor.transpose(bankt[:, q * P:(q + 1) * P], src[:, q * P:(q + 1) * P], ident[:, :])
                mm.then_inc(feat[kind], 1)

            def layer1(g, m, gen):
                if m == 0:
                    pe.wait_ge(xn_lo_r, g + 1)
                if m == 0:
                    wait(pe, y2_hi_r, 4 * g - 3)
                    wait(pe, y3_hi_r, 4 * g - 5)
                if m == 1:
                    wait(pe, y2_hi_r, 4 * g - 1)
                if m == 2:
                    pe.wait_ge(y1_r, 4 * g + 1)
                if m == 3:
                    pe.wait_ge(y1_r, 4 * g + 2)
                    wait(pe, y3_hi_r, 4 * g - 3)
                split_mm(B1[m][0][:, :], 0, 0, m, xn_hi[:, :], xn_lo[:, :], True, True, gen)
                split_mm(B1[m][1][:, :], 1, 0, m, xn_hi[:, :], xn_lo[:, :], True, True, gen).then_inc(l1_mm, 1)

            def layer2(g, m, gen):
                if m == 0:
                    wait(pe, y3_hi_r, 4 * g)
                    pe.wait_ge(y1_r, 4 * g + 4)
                if m == 1:
                    wait(pe, l4_out, g)
                for k in range(KT):
                    if m == 0:
                        pe.wait_ge(y1_hi_r, 4 * g + k + 1)
                        pe.wait_ge(y1_lo_r, 4 * g + k + 1)
                    mm = split_mm(B2[m][:, :], 2, k, m, y1_hi[:, k, :], y1_lo[:, k, :], k == 0, k == KT - 1, gen)
                mm.then_inc(l2_mm, 1)

            def layer3(g, m, gen, overlap):
                if overlap and m:
                    pe.wait_ge(y1_r, 4 * g + 4 + min(m + 1, 3))
                for k in range(KT):
                    if m == 0:
                        if k == 0:
                            pe.wait_ge(y2_hi_r, 4 * g + 4)
                        pe.wait_ge(y2_lo_pool if k % 2 == 0 else y2_lo_dve, 2 * g + k // 2 + 1)
                    mm = split_mm(B3[m][:, :], 3, k, m, y2_hi[:, k, :], y2_lo[:, k, :], k == 0, k == KT - 1, gen)
                mm.then_inc(l3_mm, 1)

            def layer4(g, gen):
                for k in range(KT):
                    pe.wait_ge(y3_hi_r, 4 * g + max(k, 1) + 1)
                    pe.wait_ge(y3_lo_pool if k % 2 == 0 else y3_lo_dve, 2 * g + k // 2 + 1)
                    mm = split_mm(B4[:, :], 4, k, 0, y3_hi[:, k, :], y3_lo[:, k, :], k == 0, k == KT - 1, gen)
                mm.then_inc(l4_mm, 1)

            def x_times_b(c):
                pe.wait_ge(xn2_r, c + 1)
                for b in range(SEQS):
                    mm = nc.tensor.matmul(MI[:, 0:HCOLS], b_pad[:, b, :], xn2[:, b * HCOLS:(b + 1) * HCOLS],
                                          start=b == 0, stop=b == SEQS - 1)
                mm.then_inc(xb_mm, 1)

            def scan_step(n, c, t, first_pass=False):
                s = n * CSTEPS + t
                if t == 0:
                    if first_pass:
                        pe.wait_ge(xb_r, c + 1)
                    wait(pe, step_h, s)
                    nc.tensor.matmul(SC[:, 0:HCOLS], ident[:, :], cols(xb_all, c, HCOLS), start=True, stop=False,
                                     skip_group_check=True)
                wait(pe, step_h, s)
                off = c * HCOLS + t * BLOCKS
                nc.tensor.matmul(SC[:, t * BLOCKS:(t + 1) * BLOCKS], a_blk[:, :], h_all[:, bass.ds(off, BLOCKS)],
                                 start=False, stop=t == CSTEPS - 1, skip_group_check=True).then_inc(step_mm, 1)

            def attention(gb, c):
                pe.wait_ge(step_h, (gb + CHUNKS + 1) * CSTEPS)
                wait(pe, x2_r, gb)
                for b in range(SEQS):
                    mm = nc.tensor.matmul(MI[:, b * HCOLS:(b + 1) * HCOLS], cw_pad[:, b, :],
                                          h_all[:, bass.ds(c * HCOLS + BLOCKS, HCOLS)], start=True, stop=True)
                mm.then_inc(att_mm, 1)

            def turn(phase, k, g, gen, nxt, scan, mid):
                def step(t):
                    if scan is not None:
                        scan_step(scan[0], scan[1], t, phase == 0)
                if nxt:
                    if phase == 0:
                        to_tokens("f", lnin, FR, g + 1, ld_x, 16 * (k + 2))
                    else:
                        to_tokens("f", lnin, FR, g + 1, x2_r, g + 2 - CHUNKS)
                layer2(g, 0, gen)
                step(0)
                if mid is not None:
                    to_tokens("m", x1c, MI, mid, l4_out, mid + 1)
                layer2(g, 1, gen)
                step(1)
                if nxt:
                    to_features("f", xnt_f, FR, g + 1)
                layer2(g, 2, gen)
                step(2)
                if mid is not None:
                    to_features("m", xnt_m, MI, mid)
                layer2(g, 3, gen)
                step(3)
                if nxt:
                    layer1(g + 1, 0, gen)
                    layer1(g + 1, 1, gen)
                step(4)
                layer3(g, 0, gen, nxt)
                step(5)
                if nxt:
                    layer1(g + 1, 2, gen)
                layer3(g, 1, gen, nxt)
                step(6)
                if nxt:
                    layer1(g + 1, 3, gen)
                layer3(g, 2, gen, nxt)
                step(7)
                layer3(g, 3, gen, nxt)
                if mid is not None:
                    x_times_b(mid)
                if phase == 1 and scan is not None:
                    attention(scan[0] - CHUNKS, scan[1])
                layer4(g, gen)

            def program(gen):
                pe.wait_ge(w_hi_ready, 5)
                if gen:
                    pe.wait_ge(w_lo_ready, 1)
                for m in range(KT):
                    layer1(0, m, gen)
                turn(0, 0, 0, gen, True, None, None)
                turn(0, 1, 1, gen, True, None, 0)
                turn(0, 2, 2, gen, True, (0, 0), 1)
                with pe.Fori(3, CHUNKS - 1) as k:
                    turn(0, k, k, gen, True, (k - 2, k - 2), k - 1)
                last = CHUNKS - 1
                turn(0, last, last, gen, False, (last - 2, last - 2), last - 1)
                to_tokens("m", x1c, MI, last, l4_out, last + 1)
                for t in range(CSTEPS):
                    scan_step(last - 1, last - 1, t, True)
                to_features("m", xnt_m, MI, last)
                x_times_b(last)
                for t in range(CSTEPS):
                    scan_step(last, last, t, True)
                def round_(r):
                    gb = r * CHUNKS
                    pe.wait_ge(ends_r, r + 1)
                    for t in range(CSTEPS):
                        scan_step(gb + CHUNKS, 0, t)
                    attention(gb, 0)
                    to_tokens("f", lnin, FR, gb + CHUNKS, x2_r, gb + 1)
                    for t in range(CSTEPS):
                        scan_step(gb + CHUNKS + 1, 1, t)
                    to_features("f", xnt_f, FR, gb + CHUNKS)
                    attention(gb + 1, 1)
                    for m in range(KT):
                        layer1(gb + CHUNKS, m, gen)
                    with pe.Fori(0, CHUNKS - 2) as k:
                        turn(1, k, gb + k + CHUNKS, gen, True, (gb + k + CHUNKS + 2, k + 2), None)
                    turn(1, CHUNKS - 2, gb + 2 * CHUNKS - 2, gen, True, None, None)
                    if isinstance(r, int):
                        pe.wait_ge(h_nes_r, 1)
                        nc.tensor.matmul(MI[0:1, 0:1], h_nes[:, :], ones[:, :], start=True, stop=True).then_inc(agree_mm, 1)
                    turn(1, CHUNKS - 1, gb + 2 * CHUNKS - 1, gen, False, None, None)

                round_(0)
                pe.wait_ge(again_r, 1)
                need = pe.value_load(again[0:1, 0:1], min_val=0, max_val=1)
                with pe.If(need != 0):
                    with pe.Fori(1, ROUNDS) as r:
                        round_(r)

            pe.wait_ge(ld_c, 48)
            to_tokens("f", lnin, FR, 0, ld_x, 16)
            pe.wait_ge(ld_a, 32)
            nc.tensor.matmul(MI[:, 0:P], ct[:, :], wout[:, :], start=True, stop=True).then_inc(cw_mm, 1)
            to_features("f", xnt_f, FR, 0)
            pe.wait_ge(ne_ready, 6)
            nc.tensor.matmul(SC[0:1, 0:1], ne_sum[:, :], ones[:, :], start=True, stop=True).then_inc(gen_mm, 1)
            pe.wait_ge(set_up, 1)
            pe.wait_ge(cw_ready, 1)
            pe.wait_ge(pool_set, 3)
            pe.wait_ge(ld_ab, 16 * SEQS)
            pe.wait_ge(gen_ready, 1)
            is_general = pe.value_load(general[0:1, 0:1], min_val=0, max_val=1)
            with pe.If(is_general == 0):
                program(False)
            with pe.If(is_general != 0):
                program(True)

        @block.vector
        def _(dve):
            def stats(kind, g, bankt, st, mv):
                dve.wait_ge(tok[kind], g + 1)
                for q in range(QT):
                    i = nc.vector.bn_stats(st[:, q, :], bankt[:, q * P:(q + 1) * P])
                i.then_inc(bns[kind], 1)
                dve.wait_ge(bns[kind], g + 1)
                nc.vector.memset(spare[:, :], 0.0)
                for q in range(QT):
                    i = nc.vector.bn_aggr(mv[:, q, :], st[:, q, :])
                i.then_inc(var[kind], 1)

            def normalise(kind, g, bankt, mv, rs, out):
                dve.wait_ge(rstd[kind], g + 1)
                wait(dve, feat[kind], g)
                for q in range(QT):
                    i = nc.vector.tensor_scalar(out[:, q * P:(q + 1) * P], bankt[:, q * P:(q + 1) * P],
                                                mv[:, q, 0:1], rs[:, q:q + 1], ALU.subtract, ALU.mult)
                i.then_inc(normed[kind], 1)

            def xn_low(g):
                dve.wait_ge(xn_hi_r, g + 1)
                nc.vector.tensor_tensor(xn_lo[:, :], FR[:, :], xn_hi[:, :].bitcast(F32), ALU.subtract).then_inc(xn_lo_r, 1)

            def layer1(g, m):
                dve.wait_ge(th_r, 4 * g + m + 1)
                wait(dve, y1_r, 4 * g + m - 1)
                nc.vector.scalar_tensor_tensor(out=u[:, m % 2, :], in0=th[:, m % 2, :], scalar=1.0, in1=B1[m][0][:, :],
                                               op0=ALU.add, op1=ALU.mult).then_inc(u_r, 1)
                dve.wait_ge(u_r, 4 * g + m + 1)
                wait(dve, y1_lo_r, 4 * g - 3 + m)
                nc.vector.scalar_tensor_tensor(out=y1[:, m, :], in0=B1[m][1][:, :], scalar=s12h[:, m:m + 1],
                                               in1=u[:, m % 2, :], op0=ALU.mult, op1=ALU.mult).then_inc(y1_r, 1)
                dve.wait_ge(y1_r, 4 * g + m + 1)
                wait(dve, l2_mm, 4 * g)
                nc.vector.tensor_copy(y1_hi[:, m, :], y1[:, m, :]).then_inc(y1_hi_r, 1)

            def low(g, k, hi_r, y, y_hi, y_lo, out_sem):
                dve.wait_ge(hi_r, 4 * g + k + 1)
                nc.vector.tensor_tensor(y_lo[:, k, :], y[:, k, :], y_hi[:, k, :].bitcast(F32), ALU.subtract).then_inc(out_sem, 1)

            def layer4(phase, g, c):
                dve.wait_ge(l4_mm, g + 1)
                if phase == 0:
                    dve.wait_ge(ld_xall, 16)
                    wait(dve, x1_saved, 16 * g)
                    wait(dve, tok["m"], g)
                    res, dst = cols(x_all, c), x1c[:, :]
                else:
                    gb = g - CHUNKS
                    dve.wait_ge(x2_saved, 16 * (gb + 1))
                    wait(dve, out_sem, 16 * gb)
                    res, dst = cols(x2_all, c), outb[:, :]
                nc.vector.scalar_tensor_tensor(out=dst, in0=B4[:, :], scalar=s3h[:, :], in1=res,
                                               op0=ALU.mult, op1=ALU.add).then_inc(l4_out, 1)

            def attention(gb, c):
                dve.wait_ge(att_mm, gb + 1)
                wait(dve, x2_saved, 16 * gb)
                dve.wait_ge(tok["f"], gb + CHUNKS)
                nc.vector.scalar_tensor_tensor(out=lnin[:, :], in0=MI[:, :], scalar=sc[:, 4 * KT + 1:4 * KT + 2],
                                               in1=cols(x_all, c), op0=ALU.add, op1=ALU.add).then_inc(x2_r, 1)

            def turn(phase, k, g, nxt, att, mid):
                if nxt:
                    stats("f", g + 1, FR, st_f, mv_f)
                if mid is not None:
                    stats("m", mid, MI, st_m, mv_m)
                if nxt:
                    normalise("f", g + 1, FR, mv_f, rs_f, xnt_f)
                low(g, 1, y2_hi_r, y23, y2_hi, y2_lo, y2_lo_dve)
                if mid is not None:
                    normalise("m", mid, MI, mv_m, rs_m, xnt_m)
                if nxt:
                    xn_low(g + 1)
                low(g, 3, y2_hi_r, y23, y2_hi, y2_lo, y2_lo_dve)
                if nxt:
                    for m in range(KT):
                        layer1(g + 1, m)
                low(g, 1, y3_hi_r, y23, y3_hi, y3_lo, y3_lo_dve)
                low(g, 3, y3_hi_r, y23, y3_hi, y3_lo, y3_lo_dve)
                if att is not None:
                    attention(att[0], att[1])
                layer4(phase, g, k)

            nc.vector.memset(h_all[:, 0:BLOCKS], 0.0)
            nc.vector.memset(ones[:, :], 1.0)
            nc.vector.memset(epsc[:, :], EPS)
            nc.vector.memset(mhalf[:, :], -0.5).then_inc(set_up, 1)
            stats("f", 0, FR, st_f, mv_f)
            for i in range(2):
                dve.wait_ge(ld_w[i], 16)
                nc.vector.tensor_copy(w_hi[:, WOFF[i]:WOFF[i + 1]], w_raw[:, WOFF[i]:WOFF[i + 1]]).then_inc(w_hi_ready, 1)
            normalise("f", 0, FR, mv_f, rs_f, xnt_f)
            xn_low(0)
            for i in range(2, 5):
                dve.wait_ge(ld_w[i], 16)
                nc.vector.tensor_copy(w_hi[:, WOFF[i]:WOFF[i + 1]], w_raw[:, WOFF[i]:WOFF[i + 1]]).then_inc(w_hi_ready, 1)
            dve.wait_ge(w_hi_ready, 5)
            for i in range(5):
                nc.vector.scalar_tensor_tensor(out=w_ne[:, 0:WCOLS[i]], in0=w_raw[:, WOFF[i]:WOFF[i + 1]], scalar=0.0,
                                               in1=w_hi[:, WOFF[i]:WOFF[i + 1]].bitcast(F32), op0=ALU.add,
                                               op1=ALU.not_equal, accum_out=ne_cnt[:, i:i + 1]).then_inc(ne_ready, 1)
                dve.wait_ge(ne_ready, i + 1)
            nc.vector.reduce_sum(ne_sum[:, :], ne_cnt[:, :], axis=mybir.AxisListType.X).then_inc(ne_ready, 1)
            dve.wait_ge(gen_mm, 1)
            nc.vector.tensor_scalar(general[:, :], SC[0:1, 0:1], 0.0, None, ALU.is_gt).then_inc(gen_ready, 1)
            dve.wait_ge(ld_sc, 16)
            nc.vector.tensor_scalar(s1h[:, :], sc[:, 0:KT], 0.5, None, ALU.mult).then_inc(set_up, 1)
            nc.vector.tensor_scalar(s3h[:, :], sc[:, 4 * KT:4 * KT + 1], 0.5, None, ALU.mult).then_inc(set_up, 1)
            dve.wait_ge(set_up, 3)
            nc.vector.tensor_tensor(s12h[:, :], s1h[:, :], sc[:, KT:2 * KT], ALU.mult).then_inc(set_up, 1)
            dve.wait_ge(set_up, 4)
            dve.wait_ge(cw_mm, 1)
            dve.wait_ge(ld_c, 48)
            for b in range(SEQS):
                i = nc.vector.tensor_scalar(cw_pad[:, b, :], MI[:, 0:P], mask[:, b:b + 1], None, ALU.mult)
            i.then_inc(cw_ready, 1)

            for m in range(KT):
                layer1(0, m)
            turn(0, 0, 0, True, None, None)
            turn(0, 1, 1, True, None, 0)
            with dve.Fori(2, CHUNKS - 1) as k:
                turn(0, k, k, True, None, k - 1)
            last = CHUNKS - 1
            turn(0, last, last, False, None, last - 1)
            stats("m", last, MI, st_m, mv_m)
            normalise("m", last, MI, mv_m, rs_m, xnt_m)
            def round_(r):
                gb = r * CHUNKS
                dve.wait_ge(step_h, (gb + CHUNKS) * CSTEPS)
                nc.vector.tensor_copy(h_all[:, 1:BLOCKS], h_all[:, STEPS * BLOCKS:STEPS * BLOCKS + BLOCKS - 1]).then_inc(ends_r, 1)
                attention(gb, 0)
                stats("f", gb + CHUNKS, FR, st_f, mv_f)
                normalise("f", gb + CHUNKS, FR, mv_f, rs_f, xnt_f)
                xn_low(gb + CHUNKS)
                attention(gb + 1, 1)
                for m in range(KT):
                    layer1(gb + CHUNKS, m)
                turn(1, 0, gb + CHUNKS, True, (gb + 2, 2), None)
                with dve.Fori(1, CHUNKS - 2) as k:
                    turn(1, k, gb + k + CHUNKS, True, (gb + k + 2, k + 2), None)
                if isinstance(r, int):
                    dve.wait_ge(step_h, 2 * CHUNKS * CSTEPS)
                    nc.vector.tensor_tensor(h_ne[:, 1:BLOCKS], h_all[:, 1:BLOCKS],
                                            h_all[:, STEPS * BLOCKS:STEPS * BLOCKS + BLOCKS - 1],
                                            ALU.not_equal).then_inc(h_ne_r, 1)
                    dve.wait_ge(h_ne_r, 1)
                    nc.vector.reduce_sum(h_nes[:, :], h_ne[:, 1:BLOCKS], axis=mybir.AxisListType.X).then_inc(h_nes_r, 1)
                turn(1, CHUNKS - 2, gb + 2 * CHUNKS - 2, True, None, None)
                if isinstance(r, int):
                    dve.wait_ge(agree_mm, 1)
                    nc.vector.tensor_scalar(again[:, :], MI[0:1, 0:1], 0.0, None, ALU.is_gt).then_inc(again_r, 1)
                turn(1, CHUNKS - 1, gb + 2 * CHUNKS - 1, False, None, None)

            round_(0)
            dve.wait_ge(again_r, 1)
            need = dve.value_load(again[0:1, 0:1], min_val=0, max_val=1)
            with dve.If(need != 0):
                with dve.Fori(1, ROUNDS) as r:
                    round_(r)

        @block.scalar
        def _(act):
            def front(g):
                act.wait_ge(feat["f"], g + 1)
                wait(act, l1_mm, 4 * g)
                nc.scalar.copy(xn_hi[:, :], FR[:, :]).then_inc(xn_hi_r, 1)

            def layer1(g, m):
                act.wait_ge(l1_mm, 4 * g + m + 1)
                wait(act, u_r, 4 * g + m - 1)
                nc.scalar.activation(th[:, m % 2, :], B1[m][0][:, :], ACT.Tanh, scale=s1h[:, m:m + 1]).then_inc(th_r, 1)

            def gelu(g, m, mm, bankt, s, y_hi, y_read, next_mm, hi_r):
                act.wait_ge(mm, 4 * g + m + 1)
                wait(act, *y_read)
                nc.scalar.activation(y23[:, m, :], bankt[:, :], ACT.Gelu, scale=s)
                wait(act, *next_mm)
                nc.scalar.activation(y_hi[:, m, :], bankt[:, :], ACT.Gelu, scale=s).then_inc(hi_r, 1)

            def gelu2(g, m):
                gelu(g, m, l2_mm, B2[m], sc[:, 2 * KT + m:2 * KT + m + 1], y2_hi,
                     (y3_lo_pool if m % 2 == 0 else y3_lo_dve, 2 * g + m // 2 - 1), (l3_mm, 4 * g), y2_hi_r)

            def gelu3(g, m):
                gelu(g, m, l3_mm, B3[m], sc[:, 3 * KT + m:3 * KT + m + 1], y3_hi,
                     (y2_lo_pool if m % 2 == 0 else y2_lo_dve, 2 * g + m // 2 + 1), (l4_mm, g), y3_hi_r)

            def middle_copy(c):
                act.wait_ge(feat["m"], c + 1)
                nc.scalar.copy(xn2[:, :], MI[:, :]).then_inc(xn2_r, 1)

            def xb_copy(c):
                act.wait_ge(xb_mm, c + 1)
                nc.scalar.copy(cols(xb_all, c, HCOLS), MI[:, 0:HCOLS]).then_inc(xb_r, 1)

            def scan_step(n, c, t):
                act.wait_ge(step_mm, n * CSTEPS + t + 1)
                nc.scalar.activation(h_all[:, bass.ds(c * HCOLS + (t + 1) * BLOCKS, BLOCKS)],
                                     SC[:, t * BLOCKS:(t + 1) * BLOCKS], ACT.Tanh).then_inc(step_h, 1)

            def turn(g, nxt, scan, mid):
                def step(t):
                    if scan is not None:
                        scan_step(scan[0], scan[1], t)
                gelu2(g, 0)
                step(0)
                gelu2(g, 1)
                step(1)
                if nxt:
                    front(g + 1)
                gelu2(g, 2)
                step(2)
                if mid is not None:
                    middle_copy(mid)
                gelu2(g, 3)
                step(3)
                if nxt:
                    layer1(g + 1, 0)
                    layer1(g + 1, 1)
                step(4)
                gelu3(g, 0)
                step(5)
                if nxt:
                    layer1(g + 1, 2)
                gelu3(g, 1)
                step(6)
                if nxt:
                    layer1(g + 1, 3)
                gelu3(g, 2)
                step(7)
                gelu3(g, 3)
                if mid is not None:
                    xb_copy(mid)

            front(0)
            act.wait_ge(ld_sc, 16)
            act.wait_ge(set_up, 4)
            for m in range(KT):
                layer1(0, m)
            turn(0, True, None, None)
            turn(1, True, None, 0)
            with act.Fori(2, CHUNKS - 1) as k:
                turn(k, True, (k - 2, k - 2), k - 1)
            last = CHUNKS - 1
            turn(last, False, (last - 2, last - 2), last - 1)
            for t in range(CSTEPS):
                scan_step(last - 1, last - 1, t)
            middle_copy(last)
            xb_copy(last)
            for t in range(CSTEPS):
                scan_step(last, last, t)
            def round_(r):
                gb = r * CHUNKS
                for t in range(CSTEPS):
                    scan_step(gb + CHUNKS, 0, t)
                for t in range(CSTEPS):
                    scan_step(gb + CHUNKS + 1, 1, t)
                front(gb + CHUNKS)
                for m in range(KT):
                    layer1(gb + CHUNKS, m)
                with act.Fori(0, CHUNKS - 2) as k:
                    turn(gb + k + CHUNKS, True, (gb + k + CHUNKS + 2, k + 2), None)
                turn(gb + 2 * CHUNKS - 2, True, None, None)
                turn(gb + 2 * CHUNKS - 1, False, None, None)

            round_(0)
            act.wait_ge(again_r, 1)
            need = act.value_load(again[0:1, 0:1], min_val=0, max_val=1)
            with act.If(need != 0):
                with act.Fori(1, ROUNDS) as r:
                    round_(r)

        @block.gpsimd
        def _(pool):
            def inverse_std(kind, g, mv, ve, rs):
                pool.wait_ge(var[kind], g + 1)
                pool.tensor_tensor(ve[:, :], mv[:, :, 1], epsc[:, :], ALU.add).then_inc(veps[kind], 1)
                pool.wait_ge(veps[kind], g + 1)
                wait(pool, normed[kind], g)
                pool.tensor_tensor(rs[:, :], ve[:, :], mhalf[:, :], ALU.pow).then_inc(rstd[kind], 1)

            def low(g, k, hi_r, per, y, y_hi, y_lo, out_sem, free):
                pool.wait_ge(hi_r, 4 * g + k + 1)
                wait(pool, *free)
                pool.tensor_tensor(y_lo[:, k, :], y[:, k, :], y_hi[:, k, :].bitcast(F32), ALU.subtract).then_inc(out_sem, 1)

            def layer1(g):
                for m in range(KT):
                    low(g, m, y1_hi_r, 4, y1, y1_hi, y1_lo, y1_lo_r, (l2_mm, 4 * g))

            def turn(g, nxt, mid):
                if nxt:
                    inverse_std("f", g + 1, mv_f, ve_f, rs_f)
                if mid is not None:
                    inverse_std("m", mid, mv_m, ve_m, rs_m)
                low(g, 0, y2_hi_r, 2, y23, y2_hi, y2_lo, y2_lo_pool, (l3_mm, 4 * g))
                low(g, 2, y2_hi_r, 2, y23, y2_hi, y2_lo, y2_lo_pool, (l3_mm, 4 * g))
                if nxt:
                    layer1(g + 1)
                low(g, 0, y3_hi_r, 2, y23, y3_hi, y3_lo, y3_lo_pool, (l4_mm, g))
                low(g, 2, y3_hi_r, 2, y23, y3_hi, y3_lo, y3_lo_pool, (l4_mm, g))

            pool.memset(a_blk[:, :], 0.0).then_inc(pool_set, 1)
            pool.wait_ge(set_up, 1)
            inverse_std("f", 0, mv_f, ve_f, rs_f)
            pool.memset(b_pad[:, :, :], 0.0).then_inc(pool_set, 1)
            pool.wait_ge(pool_set, 2)
            pool.wait_ge(ld_c, 48)
            for b in range(SEQS):
                i = pool.tensor_copy(b_pad[:, b, b * STATES:(b + 1) * STATES], b_sb[:, :])
            i.then_inc(pool_set, 1)
            pool.wait_ge(gen_ready, 1)
            is_general = pool.value_load(general[0:1, 0:1], min_val=0, max_val=1)
            with pool.If(is_general != 0):
                pool.tensor_tensor(w_lo[:, :], w_raw[:, :], w_hi[:, :].bitcast(F32), ALU.subtract).then_inc(w_lo_ready, 1)
            layer1(0)
            turn(0, True, None)
            turn(1, True, 0)
            with pool.Fori(2, CHUNKS - 1) as k:
                turn(k, True, k - 1)
            last = CHUNKS - 1
            turn(last, False, last - 1)
            inverse_std("m", last, mv_m, ve_m, rs_m)
            def round_(r):
                gb = r * CHUNKS
                inverse_std("f", gb + CHUNKS, mv_f, ve_f, rs_f)
                layer1(gb + CHUNKS)
                with pool.Fori(0, CHUNKS - 2) as k:
                    turn(gb + k + CHUNKS, True, None)
                turn(gb + 2 * CHUNKS - 2, True, None)
                turn(gb + 2 * CHUNKS - 1, False, None)

            round_(0)
            pool.wait_ge(again_r, 1)
            need = pool.value_load(again[0:1, 0:1], min_val=0, max_val=1)
            with pool.If(need != 0):
                with pool.Fori(1, ROUNDS) as r:
                    round_(r)

        @block.sync
        def _(sp):
            sp.dma_start(lnin[:, :], xT[:, 0:N]).then_inc(ld_x, 16)
            sp.dma_start(ident[:, :], ident_d).then_inc(ld_c, 16)
            for i, w in enumerate((w1T, w2T)):
                sp.dma_start(w_raw[:, WOFF[i]:WOFF[i + 1]], w).then_inc(ld_w[i], 16)
            sp.dma_start(mask[:, :], mask_d).then_inc(ld_c, 16)
            sp.dma_start(b_sb[:, :], Bm).then_inc(ld_c, 16)
            sp.dma_start(ct[:, :], CTrep).then_inc(ld_a, 16)
            sp.dma_start(wout[:, :], WoutT).then_inc(ld_a, 16)
            sp.dma_start(sc[:, :], scales).then_inc(ld_sc, 16)
            for i, w in ((2, h1T), (3, h2T), (4, w3T)):
                sp.dma_start(w_raw[:, WOFF[i]:WOFF[i + 1]], w).then_inc(ld_w[i], 16)
            sp.wait_ge(pool_set, 1)
            sp.dma_start(x_all[:, :], xT).then_inc(ld_xall, 16)
            for b in range(SEQS):
                rows = slice(b * STATES, (b + 1) * STATES)
                sp.dma_start(a_blk[rows, rows], AT).then_inc(ld_ab, 16)
            for c in range(1, 2):
                sp.wait_ge(tok["f"], c)
                sp.dma_start(lnin[:, :], xT[:, c * N:(c + 1) * N]).then_inc(ld_x, 16)
            with sp.Fori(0, CHUNKS - 2) as k:
                sp.wait_ge(tok["f"], k + 2)
                sp.dma_start(lnin[:, :], xT[:, bass.ds(k * N + 2 * N, N)]).then_inc(ld_x, 16)
                sp.wait_ge(l4_out, k + 1)
                sp.dma_start(cols(x_all, k), x1c[:, :]).then_inc(x1_saved, 16)
            for k in (CHUNKS - 2, CHUNKS - 1):
                sp.wait_ge(l4_out, k + 1)
                sp.dma_start(cols(x_all, k), x1c[:, :]).then_inc(x1_saved, 16)
            def round_(r):
                gb = r * CHUNKS
                for c in range(2):
                    sp.wait_ge(x2_r, gb + c + 1)
                    sp.dma_start(cols(x2_all, c), lnin[:, :]).then_inc(x2_saved, 16)
                with sp.Fori(0, CHUNKS - 2) as k:
                    sp.wait_ge(x2_r, gb + k + 3)
                    sp.dma_start(cols(x2_all, k + 2), lnin[:, :]).then_inc(x2_saved, 16)
                    sp.wait_ge(l4_out, gb + k + CHUNKS + 1)
                    sp.dma_start(outT[:, bass.ds(k * N, N)], outb[:, :]).then_inc(out_sem, 16)
                for k in (CHUNKS - 2, CHUNKS - 1):
                    sp.wait_ge(l4_out, gb + k + CHUNKS + 1)
                    sp.dma_start(outT[:, k * N:(k + 1) * N], outb[:, :]).then_inc(out_sem, 16)

            round_(0)
            sp.wait_ge(again_r, 1)
            need = sp.value_load(again[0:1, 0:1], min_val=0, max_val=1)
            with sp.If(need != 0):
                with sp.Fori(1, ROUNDS) as r:
                    round_(r)
                sp.wait_ge(out_sem, 16 * CHUNKS * ROUNDS)
            with sp.If(need == 0):
                sp.wait_ge(out_sem, 16 * CHUNKS)

def kernel(**inputs):
    import numpy as np
    import concourse.bacc as _bacc
    from concourse import mybir as _mybir
    from concourse.bass_utils import run_bass_kernel_spmd as _run

    v = {k[3:]: np.asarray(a) for k, a in inputs.items()}
    tiles = lambda w: np.ascontiguousarray(w.T.reshape(-1, P, w.shape[0]).transpose(1, 0, 2)).reshape(P, -1)
    col = lambda s: s.reshape(-1, P).T
    arrays = {
        "xT": np.ascontiguousarray(v["attn_x"].reshape(SEQS, BLOCKS, CHUNKS, CSTEPS, P).transpose(4, 2, 0, 3, 1)).reshape(P, -1),
        "w1T": tiles(v["ffn_w1_w"]), "w2T": tiles(v["ffn_w2_w"]), "h1T": tiles(v["ffn_h1_w"]),
        "h2T": tiles(v["ffn_h2_w"]), "w3T": tiles(v["ffn_w3_w"]),
        "scales": np.ascontiguousarray(np.concatenate(
            [col(v[n]) for n in ("ffn_w1_s", "ffn_w2_s", "ffn_h1_s", "ffn_h2_s", "ffn_w3_s", "attn_b_out")], axis=1)),
        "AT": np.ascontiguousarray(v["attn_A"].T),
        "Bm": np.ascontiguousarray(v["attn_B"]),
        "CTrep": np.ascontiguousarray(np.tile(v["attn_C"].T, (1, SEQS))),
        "WoutT": np.ascontiguousarray(v["attn_W_out"].T),
        "ident": np.eye(P, dtype=np.float32),
        "mask": np.kron(np.eye(SEQS, dtype=np.float32), np.ones((STATES, 1), np.float32)),
    }
    nc = _bacc.Bacc("TRN2", target_bir_lowering=False, num_devices=1)
    args = [nc.dram_tensor(f"in_{n}", a.shape, _mybir.dt.from_np(a.dtype), kind="ExternalInput").ap()
            for n, a in arrays.items()]
    out = nc.dram_tensor("out", (P, CHUNKS * N), F32, kind="ExternalOutput").ap()
    build(nc, *args, out)
    r = _run(nc, [{f"in_{n}": a for n, a in arrays.items()}], core_ids=[0])
    o = np.asarray(r.results[0]["out"]).reshape(P, CHUNKS, SEQS, CSTEPS, BLOCKS)
    return np.ascontiguousarray(o.transpose(2, 4, 1, 3, 0)).reshape(SEQS, LENGTH, P)
```

```python
from contextlib import ExitStack

import concourse.bass as bass
from concourse import mybir

F32 = mybir.dt.float32
F32R = mybir.dt.float32r
I32 = mybir.dt.int32
ALU = mybir.AluOpType
ACT = mybir.ActivationFunctionType

P = 128
SEQS = 8
LENGTH = 512
STATES = 16
BLOCKS = 8
ROUNDS = BLOCKS - 1
STEPS = LENGTH // BLOCKS
CHUNKS = 8
CSTEPS = STEPS // CHUNKS
HCOLS = CSTEPS * BLOCKS
N = SEQS * HCOLS
FIRST = 2
FIRST_PASS = CHUNKS - FIRST
HID = 512
KT = HID // P
QT = N // P
EPS = 1e-5


def wait(engine, sem, value):
    if isinstance(value, int) and value <= 0:
        return
    engine.wait_ge(sem, value)


def build(nc, xT, w1T, w2T, h1T, h2T, w3T, scales, AT, Bm, CTrep, WoutT, ident_d, mask_d, outT):
    with ExitStack() as ctx:
        def sb(name, shape, dt=F32):
            return ctx.enter_context(nc.sbuf_tensor(name, shape, dt))

        def bank(name):
            return ctx.enter_context(nc.psum_tensor(name, [P, N], F32))

        def sem(name):
            return ctx.enter_context(nc.semaphore(name))

        WCOLS = [HID, HID, KT * HID, KT * HID, KT * P]
        WOFF = [sum(WCOLS[:i]) for i in range(6)]
        HALF = KT * HID // 2
        PIECES = [(0, HID), (HID, HID)] + [(WOFF[2] + i * HALF, HALF) for i in range(4)] + [(WOFF[4], KT * P)]
        w_raw = sb("w_raw", [P, WOFF[5]])
        w_hi = sb("w_hi", [P, WOFF[5]], F32R)
        w_lo = sb("w_lo", [P, WOFF[5]], F32R)
        ne_cnt = sb("ne_cnt", [P, len(PIECES)])
        ne_sum = sb("ne_sum", [P, 1])
        sc = sb("sc", [P, 4 * KT + 2])
        s1h = sb("s1h", [P, KT])
        s12h = sb("s12h", [P, KT])
        s3h = sb("s3h", [P, 1])
        ident = sb("ident", [P, P])
        mask = sb("mask", [P, SEQS])
        ones = sb("ones", [P, 1])
        a_blk = sb("a_blk", [P, P])
        b_sb = sb("b_sb", [P, STATES])
        b_pad = sb("b_pad", [P, SEQS, P])
        ct = sb("ct", [P, P])
        wout = sb("wout", [P, P])
        cw = sb("cw", [P, P])
        cw_pad = sb("cw_pad", [P, SEQS, P])
        x_all = sb("x_all", [P, CHUNKS * N])
        x2_all = sb("x2_all", [P, CHUNKS * N])
        lnin = sb("lnin", [P, N])
        x1c = sb("x1c", [P, N])
        outb = sb("outb", [P, N])
        st_f = sb("st_f", [P, QT, 6])
        st_m = sb("st_m", [P, QT, 6])
        mv_f = sb("mv_f", [P, QT, 2])
        mv_m = sb("mv_m", [P, QT, 2])
        ve_f = sb("ve_f", [P, QT])
        ve_m = sb("ve_m", [P, QT])
        rs_f = sb("rs_f", [P, QT])
        rs_m = sb("rs_m", [P, QT])
        spare = sb("spare", [P, 1])
        mhalf = sb("mhalf", [P, QT])
        epsc = sb("epsc", [P, QT])
        xnt_f = sb("xnt_f", [P, N])
        xnt_m = sb("xnt_m", [P, N])
        xn_hi = sb("xn_hi", [P, N], F32R)
        xn_lo = sb("xn_lo", [P, N], F32R)
        xn2 = sb("xn2", [P, N])
        xb_all = sb("xb_all", [P, CHUNKS * HCOLS])
        h_all = sb("h_all", [P, BLOCKS + STEPS * BLOCKS])
        h_ne = sb("h_ne", [P, BLOCKS])
        h_nes = sb("h_nes", [P, 1])
        again = sb("again", [1, 1], I32)
        general = sb("general", [1, 1], I32)
        th = sb("th", [P, 2, N])
        u = sb("u", [P, 2, N])
        y1 = sb("y1", [P, KT, N])
        w_ne = y1[:, :, :].rearrange("p k n -> p (k n)")
        y23 = sb("y23", [P, KT, N])
        y1_hi = sb("y1_hi", [P, KT, N], F32R)
        y1_lo = sb("y1_lo", [P, KT, N], F32R)
        y2_hi = sb("y2_hi", [P, KT, N], F32R)
        y2_lo = sb("y2_lo", [P, KT, N], F32R)
        y3_hi = sb("y3_hi", [P, KT, N], F32R)
        y3_lo = sb("y3_lo", [P, KT, N], F32R)

        F = [bank(f"F{i}") for i in range(5)]
        FR = bank("FR")
        MI = bank("MI")
        SC = bank("SC")
        B2 = [F[0], F[1], F[2], F[3]]
        B1 = [(F[4], F[0]), (F[1], F[2]), (F[4], F[0]), (F[2], F[3])]
        B3 = [F[3], F[1], F[4], F[0]]
        B4 = F[1]

        ld_w = [sem(f"ld_w{i}") for i in range(len(PIECES))]
        ld_sc = sem("ld_sc")
        ld_c = sem("ld_c")
        ld_a = sem("ld_a")
        ld_ab = sem("ld_ab")
        ld_x = sem("ld_x")
        ld_xall = sem("ld_xall")
        set_up = sem("set_up")
        pool_set = sem("pool_set")
        w_hi_ready = sem("w_hi_ready")
        w_lo1_ready = sem("w_lo1_ready")
        w_lo_ready = sem("w_lo_ready")
        ne_ready = sem("ne_ready")
        gen_mm = sem("gen_mm")
        gen_ready = sem("gen_ready")
        cw_mm = sem("cw_mm")
        cw_ready = sem("cw_ready")
        tok = {k: sem(f"tok_{k}") for k in "fm"}
        bns = {k: sem(f"bns_{k}") for k in "fm"}
        var = {k: sem(f"var_{k}") for k in "fm"}
        veps = {k: sem(f"veps_{k}") for k in "fm"}
        rstd = {k: sem(f"rstd_{k}") for k in "fm"}
        normed = {k: sem(f"normed_{k}") for k in "fm"}
        feat = {k: sem(f"feat_{k}") for k in "fm"}
        xn_hi_r = sem("xn_hi_r")
        xn_lo_r = sem("xn_lo_r")
        l1_mm = sem("l1_mm")
        th_r = sem("th_r")
        u_r = sem("u_r")
        y1_r = sem("y1_r")
        y1_hi_r = sem("y1_hi_r")
        y1_lo_r = sem("y1_lo_r")
        l2_mm = sem("l2_mm")
        y2_hi_r = sem("y2_hi_r")
        y2_lo_dve = sem("y2_lo_dve")
        y2_lo_pool = sem("y2_lo_pool")
        l3_mm = sem("l3_mm")
        y3_hi_r = sem("y3_hi_r")
        y3_lo_dve = sem("y3_lo_dve")
        y3_lo_pool = sem("y3_lo_pool")
        l4_mm = sem("l4_mm")
        l4_out = sem("l4_out")
        x1_saved = sem("x1_saved")
        xn2_r = sem("xn2_r")
        xb_mm = sem("xb_mm")
        xb_r = sem("xb_r")
        step_mm = sem("step_mm")
        step_h = sem("step_h")
        ends_r = sem("ends_r")
        h_ne_r = sem("h_ne_r")
        h_nes_r = sem("h_nes_r")
        agree_mm = sem("agree_mm")
        again_r = sem("again_r")
        att_mm = sem("att_mm")
        x2_r = sem("x2_r")
        x2_saved = sem("x2_saved")
        out_sem = sem("out_sem")

        block = ctx.enter_context(nc.Block())

        def wtile(w, layer, k, m):
            width = P if layer == 4 else HID
            off = WOFF[layer] + k * width + m * P
            return w[:, off:off + P]

        def cols(t, c, width=N):
            return t[:, bass.ds(c * width, width)]

        def slot(c):
            return (c - FIRST) % CHUNKS if isinstance(c, int) else c - FIRST

        @block.tensor
        def _(pe):
            def split_mm(out, layer, k, m, hi, lo, first, last, gen):
                pairs = [(w_hi, hi), (w_hi, lo)] + ([(w_lo, hi), (w_lo, lo)] if gen else [])
                for i, (w, y) in enumerate(pairs):
                    mm = nc.tensor.matmul(out, wtile(w, layer, k, m), y, start=first and i == 0,
                                          stop=last and i == len(pairs) - 1)
                return mm

            def to_tokens(kind, src, bankt, g, ready, value, att=0):
                pe.wait_ge(ready, value)
                if kind == "f":
                    wait(pe, xn_lo_r, g)
                else:
                    wait(pe, xb_r, g)
                    wait(pe, x2_r, att)
                for q in range(QT):
                    mm = nc.tensor.transpose(bankt[:, q * P:(q + 1) * P], src[:, q * P:(q + 1) * P], ident[:, :])
                mm.then_inc(tok[kind], 1)

            def to_features(kind, src, bankt, g):
                pe.wait_ge(normed[kind], g + 1)
                for q in range(QT):
                    mm = nc.tensor.transpose(bankt[:, q * P:(q + 1) * P], src[:, q * P:(q + 1) * P], ident[:, :])
                mm.then_inc(feat[kind], 1)

            def layer1(g, m, gen, late=False):
                if m == 0:
                    pe.wait_ge(xn_lo_r, g + 1)
                if late:
                    if m == 0:
                        pe.wait_ge(y3_hi_r, 4 * g)
                    if m == 1:
                        pe.wait_ge(l4_out, g)
                elif m == 0:
                    wait(pe, y2_hi_r, 4 * g - 3)
                    wait(pe, y3_hi_r, 4 * g - 5)
                elif m == 1:
                    wait(pe, y2_hi_r, 4 * g - 1)
                if m == 2:
                    pe.wait_ge(y1_r, 4 * g + 1)
                if m == 3:
                    pe.wait_ge(y1_r, 4 * g + 2)
                    if not late:
                        wait(pe, y3_hi_r, 4 * g - 3)
                split_mm(B1[m][0][:, :], 0, 0, m, xn_hi[:, :], xn_lo[:, :], True, True, gen)
                split_mm(B1[m][1][:, :], 1, 0, m, xn_hi[:, :], xn_lo[:, :], True, True, gen).then_inc(l1_mm, 1)

            def layer2(g, m, gen, beside=lambda k: None):
                if m == 0:
                    wait(pe, y3_hi_r, 4 * g)
                    pe.wait_ge(y1_r, 4 * g + 3)
                if m == 1:
                    wait(pe, l4_out, g)
                for k in range(KT):
                    if m == 0:
                        pe.wait_ge(y1_hi_r, 4 * g + k + 1)
                        pe.wait_ge(y1_lo_r, 4 * g + k + 1)
                    mm = split_mm(B2[m][:, :], 2, k, m, y1_hi[:, k, :], y1_lo[:, k, :], k == 0, k == KT - 1, gen)
                    if k == KT - 1:
                        mm.then_inc(l2_mm, 1)
                    beside(k)

            def layer3(g, m, gen, overlap):
                if overlap and m:
                    pe.wait_ge(y1_r, 4 * g + 4 + min(m + 1, 3))
                for k in range(KT):
                    if m == 0:
                        if k == 0:
                            pe.wait_ge(y2_hi_r, 4 * g + 4)
                        pe.wait_ge(y2_lo_pool if k % 2 == 0 else y2_lo_dve, 2 * g + k // 2 + 1)
                    mm = split_mm(B3[m][:, :], 3, k, m, y2_hi[:, k, :], y2_lo[:, k, :], k == 0, k == KT - 1, gen)
                mm.then_inc(l3_mm, 1)

            def layer4(g, gen):
                for k in range(KT):
                    pe.wait_ge(y3_hi_r, 4 * g + max(k, 1) + 1)
                    pe.wait_ge(y3_lo_pool if k % 2 == 0 else y3_lo_dve, 2 * g + k // 2 + 1)
                    mm = split_mm(B4[:, :], 4, k, 0, y3_hi[:, k, :], y3_lo[:, k, :], k == 0, k == KT - 1, gen)
                mm.then_inc(l4_mm, 1)

            def x_times_b(c):
                pe.wait_ge(xn2_r, c + 1)
                for b in range(SEQS):
                    mm = nc.tensor.matmul(MI[:, 0:HCOLS], b_pad[:, b, :], xn2[:, b * HCOLS:(b + 1) * HCOLS],
                                          start=b == 0, stop=b == SEQS - 1)
                mm.then_inc(xb_mm, 1)

            def scan_step(n, c, t, xb_chunks=None):
                s = n * CSTEPS + t
                if t == 0:
                    if xb_chunks is not None:
                        pe.wait_ge(xb_r, xb_chunks)
                    wait(pe, step_h, s)
                    nc.tensor.matmul(SC[:, 0:HCOLS], ident[:, :], cols(xb_all, c, HCOLS), start=True, stop=False,
                                     skip_group_check=True)
                wait(pe, step_h, s)
                off = c * HCOLS + t * BLOCKS
                nc.tensor.matmul(SC[:, t * BLOCKS:(t + 1) * BLOCKS], a_blk[:, :], h_all[:, bass.ds(off, BLOCKS)],
                                 start=False, stop=t == CSTEPS - 1, skip_group_check=True).then_inc(step_mm, 1)

            def attention(gb, c):
                pe.wait_ge(step_h, (gb + FIRST_PASS + 1) * CSTEPS)
                wait(pe, x2_r, gb)
                for b in range(SEQS):
                    mm = nc.tensor.matmul(MI[:, b * HCOLS:(b + 1) * HCOLS], cw_pad[:, b, :],
                                          h_all[:, bass.ds(c * HCOLS + BLOCKS, HCOLS)], start=True, stop=True)
                mm.then_inc(att_mm, 1)

            def turn(phase, k, g, gen, nxt, scan, mid):
                def step(t):
                    if scan is not None:
                        scan_step(scan[0], scan[1], t, scan[0] + 1 if phase == 0 else None)
                if nxt:
                    if phase == 0:
                        to_tokens("f", lnin, FR, g + 1, ld_x, 16 * (k + 2))
                    else:
                        to_tokens("f", lnin, FR, g + 1, x2_r, g + 2 - CHUNKS)
                layer2(g, 0, gen)
                step(0)
                if mid is not None:
                    to_tokens("m", x1c, MI, mid, l4_out, mid + 1)
                layer2(g, 1, gen)
                step(1)
                if nxt:
                    to_features("f", xnt_f, FR, g + 1)
                layer2(g, 2, gen)
                step(2)
                if mid is not None:
                    to_features("m", xnt_m, MI, mid)
                layer2(g, 3, gen)
                step(3)
                if nxt:
                    layer1(g + 1, 0, gen)
                    layer1(g + 1, 1, gen)
                step(4)
                layer3(g, 0, gen, nxt)
                step(5)
                if nxt:
                    layer1(g + 1, 2, gen)
                layer3(g, 1, gen, nxt)
                step(6)
                if nxt:
                    layer1(g + 1, 3, gen)
                layer3(g, 2, gen, nxt)
                step(7)
                layer3(g, 3, gen, nxt)
                if mid is not None:
                    if isinstance(mid, int) and mid == 0:
                        pe.wait_ge(pool_set, 3)
                        pe.wait_ge(ld_ab, 16 * SEQS)
                    x_times_b(mid)
                if phase == 1 and scan is not None:
                    attention(scan[0] - FIRST_PASS, scan[1])
                layer4(g, gen)

            def late_turn(g, gen, mid, c):
                to_tokens("m", x1c, MI, mid, l4_out, mid + 1, att=c)
                for m in range(2):
                    def step(k):
                        if c == 0:
                            scan_step(FIRST_PASS - 1, CHUNKS - 1, KT * m + k, FIRST_PASS)
                    layer2(g, m, gen, step)
                to_features("m", xnt_m, MI, mid)
                layer2(g, 2, gen)
                x_times_b(mid)
                if c == 0:
                    pe.wait_ge(ends_r, 1)
                    pe.wait_ge(cw_ready, 1)
                layer2(g, 3, gen, lambda k: scan_step(FIRST_PASS + c, c, k, mid + 1))
                for t in range(KT, CSTEPS):
                    scan_step(FIRST_PASS + c, c, t)
                attention(c, c)
                layer3(g, 0, gen, False)
                to_tokens("f", lnin, FR, g + 1, x2_r, c + 1)
                layer3(g, 1, gen, False)
                layer3(g, 2, gen, False)
                to_features("f", xnt_f, FR, g + 1)
                layer3(g, 3, gen, False)
                layer4(g, gen)
                for m in range(KT):
                    layer1(g + 1, m, gen, late=True)
                    if c == 1:
                        for t in (2 * m, 2 * m + 1):
                            scan_step(FIRST_PASS + 2, 2, t)
                if c == 1:
                    attention(2, 2)

            def program(gen):
                pe.wait_ge(w_hi_ready, len(PIECES))
                for m in range(2, KT):
                    layer1(0, m, gen)
                if gen:
                    pe.wait_ge(w_lo_ready, 1)
                turn(0, 0, 0, gen, True, None, None)
                turn(0, 1, 1, gen, True, None, 0)
                turn(0, 2, 2, gen, True, (0, FIRST), 1)
                with pe.Fori(3, CHUNKS - 1) as k:
                    turn(0, k, k, gen, True, (k - 2, k - 2 + FIRST), k - 1)
                late_turn(CHUNKS - 1, gen, CHUNKS - 2, 0)

                def round_(r):
                    gb = r * CHUNKS
                    n = gb + FIRST_PASS
                    if isinstance(r, int):
                        late_turn(CHUNKS, gen, CHUNKS - 1, 1)
                    else:
                        pe.wait_ge(ends_r, r + 1)
                        for t in range(CSTEPS):
                            scan_step(n, 0, t)
                        attention(gb, 0)
                        to_tokens("f", lnin, FR, gb + CHUNKS, x2_r, gb + 1)
                        for t in range(CSTEPS):
                            scan_step(n + 1, 1, t)
                        to_features("f", xnt_f, FR, gb + CHUNKS)
                        attention(gb + 1, 1)
                        for m in range(KT):
                            layer1(gb + CHUNKS, m, gen, late=True)
                        turn(1, 0, gb + CHUNKS, gen, True, (n + 2, 2), None)
                    with pe.Fori(1, CHUNKS - 2) as k:
                        turn(1, k, gb + k + CHUNKS, gen, True, (n + k + 2, k + 2), None)
                    turn(1, CHUNKS - 2, gb + 2 * CHUNKS - 2, gen, True, None, None)
                    if isinstance(r, int):
                        pe.wait_ge(h_nes_r, 1)
                        nc.tensor.matmul(MI[0:1, 0:1], h_nes[:, :], ones[:, :], start=True, stop=True).then_inc(agree_mm, 1)
                    turn(1, CHUNKS - 1, gb + 2 * CHUNKS - 1, gen, False, None, None)

                round_(0)
                pe.wait_ge(again_r, 1)
                need = pe.value_load(again[0:1, 0:1], min_val=0, max_val=1)
                with pe.If(need != 0):
                    with pe.Fori(1, ROUNDS) as r:
                        round_(r)

            pe.wait_ge(ld_c, 48)
            to_tokens("f", lnin, FR, 0, ld_x, 16)
            pe.wait_ge(ld_a, 32)
            nc.tensor.matmul(MI[:, 0:P], ct[:, :], wout[:, :], start=True, stop=True).then_inc(cw_mm, 1)
            to_features("f", xnt_f, FR, 0)
            pe.wait_ge(w_hi_ready, 2)
            pe.wait_ge(w_lo1_ready, 1)
            layer1(0, 0, True)
            pe.wait_ge(ne_ready, len(PIECES) + 1)
            pe.wait_ge(set_up, 1)
            nc.tensor.matmul(SC[0:1, 0:1], ne_sum[:, :], ones[:, :], start=True, stop=True).then_inc(gen_mm, 1)
            layer1(0, 1, True)
            pe.wait_ge(gen_ready, 1)
            is_general = pe.value_load(general[0:1, 0:1], min_val=0, max_val=1)
            with pe.If(is_general == 0):
                program(False)
            with pe.If(is_general != 0):
                program(True)

        @block.vector
        def _(dve):
            def stats(kind, g, bankt, st, mv):
                dve.wait_ge(tok[kind], g + 1)
                for q in range(QT):
                    i = nc.vector.bn_stats(st[:, q, :], bankt[:, q * P:(q + 1) * P])
                i.then_inc(bns[kind], 1)
                dve.wait_ge(bns[kind], g + 1)
                nc.vector.memset(spare[:, :], 0.0)
                for q in range(QT):
                    i = nc.vector.bn_aggr(mv[:, q, :], st[:, q, :])
                i.then_inc(var[kind], 1)

            def normalise(kind, g, bankt, mv, rs, out):
                dve.wait_ge(rstd[kind], g + 1)
                wait(dve, feat[kind], g)
                for q in range(QT):
                    i = nc.vector.tensor_scalar(out[:, q * P:(q + 1) * P], bankt[:, q * P:(q + 1) * P],
                                                mv[:, q, 0:1], rs[:, q:q + 1], ALU.subtract, ALU.mult)
                i.then_inc(normed[kind], 1)

            def xn_low(g):
                dve.wait_ge(xn_hi_r, g + 1)
                nc.vector.tensor_tensor(xn_lo[:, :], FR[:, :], xn_hi[:, :].bitcast(F32), ALU.subtract).then_inc(xn_lo_r, 1)

            def layer1(g, m):
                dve.wait_ge(th_r, 4 * g + m + 1)
                wait(dve, y1_r, 4 * g + m - 1)
                nc.vector.scalar_tensor_tensor(out=u[:, m % 2, :], in0=th[:, m % 2, :], scalar=1.0, in1=B1[m][0][:, :],
                                               op0=ALU.add, op1=ALU.mult).then_inc(u_r, 1)
                dve.wait_ge(u_r, 4 * g + m + 1)
                wait(dve, y1_lo_r, 4 * g - 3 + m)
                nc.vector.scalar_tensor_tensor(out=y1[:, m, :], in0=B1[m][1][:, :], scalar=s12h[:, m:m + 1],
                                               in1=u[:, m % 2, :], op0=ALU.mult, op1=ALU.mult).then_inc(y1_r, 1)
                dve.wait_ge(y1_r, 4 * g + m + 1)
                wait(dve, l2_mm, 4 * g)
                nc.vector.tensor_copy(y1_hi[:, m, :], y1[:, m, :]).then_inc(y1_hi_r, 1)

            def low(g, k, hi_r, y, y_hi, y_lo, out_sem):
                dve.wait_ge(hi_r, 4 * g + k + 1)
                nc.vector.tensor_tensor(y_lo[:, k, :], y[:, k, :], y_hi[:, k, :].bitcast(F32), ALU.subtract).then_inc(out_sem, 1)

            def layer4(phase, g, c):
                dve.wait_ge(l4_mm, g + 1)
                if phase == 0:
                    dve.wait_ge(ld_xall, 16)
                    wait(dve, x1_saved, 16 * g)
                    wait(dve, tok["m"], g)
                    res, dst = cols(x_all, c), x1c[:, :]
                else:
                    gb = g - CHUNKS
                    dve.wait_ge(x2_saved, 16 * (gb + 1))
                    wait(dve, out_sem, 16 * gb)
                    res, dst = cols(x2_all, c), outb[:, :]
                nc.vector.scalar_tensor_tensor(out=dst, in0=B4[:, :], scalar=s3h[:, :], in1=res,
                                               op0=ALU.mult, op1=ALU.add).then_inc(l4_out, 1)

            def attention(gb, c):
                dve.wait_ge(att_mm, gb + 1)
                wait(dve, x2_saved, 16 * gb)
                dve.wait_ge(tok["f"], gb + CHUNKS)
                dve.wait_ge(x1_saved, 16 * min(slot(c) + 1, CHUNKS) if isinstance(c, int) else 16 * CHUNKS)
                nc.vector.scalar_tensor_tensor(out=lnin[:, :], in0=MI[:, :], scalar=sc[:, 4 * KT + 1:4 * KT + 2],
                                               in1=cols(x_all, slot(c)), op0=ALU.add, op1=ALU.add).then_inc(x2_r, 1)

            def restart(r):
                dve.wait_ge(step_h, (r * CHUNKS + FIRST_PASS) * CSTEPS)
                nc.vector.tensor_copy(h_all[:, 1:BLOCKS], h_all[:, STEPS * BLOCKS:STEPS * BLOCKS + BLOCKS - 1]).then_inc(ends_r, 1)

            def late_turn(phase, k, g, mid, c):
                stats("m", mid, MI, st_m, mv_m)
                normalise("m", mid, MI, mv_m, rs_m, xnt_m)
                if c == 0:
                    restart(0)
                low(g, 1, y2_hi_r, y23, y2_hi, y2_lo, y2_lo_dve)
                low(g, 3, y2_hi_r, y23, y2_hi, y2_lo, y2_lo_dve)
                attention(c, c)
                stats("f", g + 1, FR, st_f, mv_f)
                normalise("f", g + 1, FR, mv_f, rs_f, xnt_f)
                low(g, 1, y3_hi_r, y23, y3_hi, y3_lo, y3_lo_dve)
                xn_low(g + 1)
                low(g, 3, y3_hi_r, y23, y3_hi, y3_lo, y3_lo_dve)
                layer4(phase, g, k)
                for m in range(KT):
                    layer1(g + 1, m)
                if c == 1:
                    attention(2, 2)

            def turn(phase, k, g, nxt, att, mid):
                if nxt:
                    stats("f", g + 1, FR, st_f, mv_f)
                if mid is not None:
                    stats("m", mid, MI, st_m, mv_m)
                if nxt:
                    normalise("f", g + 1, FR, mv_f, rs_f, xnt_f)
                low(g, 1, y2_hi_r, y23, y2_hi, y2_lo, y2_lo_dve)
                if mid is not None:
                    normalise("m", mid, MI, mv_m, rs_m, xnt_m)
                if nxt:
                    xn_low(g + 1)
                low(g, 3, y2_hi_r, y23, y2_hi, y2_lo, y2_lo_dve)
                if nxt:
                    for m in range(KT):
                        layer1(g + 1, m)
                low(g, 1, y3_hi_r, y23, y3_hi, y3_lo, y3_lo_dve)
                low(g, 3, y3_hi_r, y23, y3_hi, y3_lo, y3_lo_dve)
                if att is not None:
                    attention(att[0], att[1])
                layer4(phase, g, k)

            def count(i):
                off, width = PIECES[i]
                dve.wait_ge(w_hi_ready, i + 1)
                wait(dve, ne_ready, i - 1)
                nc.vector.scalar_tensor_tensor(out=w_ne[:, (i % 2) * HALF:(i % 2) * HALF + width],
                                               in0=w_raw[:, off:off + width], scalar=0.0,
                                               in1=w_hi[:, off:off + width].bitcast(F32), op0=ALU.add,
                                               op1=ALU.not_equal, accum_out=ne_cnt[:, i:i + 1]).then_inc(ne_ready, 1)

            nc.vector.memset(h_all[:, 0:BLOCKS], 0.0)
            nc.vector.memset(h_all[:, FIRST * HCOLS:FIRST * HCOLS + BLOCKS], 0.0)
            nc.vector.memset(ones[:, :], 1.0)
            nc.vector.memset(epsc[:, :], EPS)
            nc.vector.memset(mhalf[:, :], -0.5).then_inc(set_up, 1)
            stats("f", 0, FR, st_f, mv_f)
            count(0)
            normalise("f", 0, FR, mv_f, rs_f, xnt_f)
            count(1)
            dve.wait_ge(ld_sc, 16)
            nc.vector.tensor_scalar(s1h[:, :], sc[:, 0:KT], 0.5, None, ALU.mult).then_inc(set_up, 1)
            nc.vector.tensor_scalar(s3h[:, :], sc[:, 4 * KT:4 * KT + 1], 0.5, None, ALU.mult).then_inc(set_up, 1)
            dve.wait_ge(set_up, 3)
            nc.vector.tensor_tensor(s12h[:, :], s1h[:, :], sc[:, KT:2 * KT], ALU.mult).then_inc(set_up, 1)
            dve.wait_ge(set_up, 4)
            count(2)
            xn_low(0)
            for i in range(3, len(PIECES)):
                count(i)
            dve.wait_ge(ne_ready, len(PIECES))
            nc.vector.reduce_sum(ne_sum[:, :], ne_cnt[:, :], axis=mybir.AxisListType.X).then_inc(ne_ready, 1)
            dve.wait_ge(gen_mm, 1)
            nc.vector.tensor_scalar(general[:, :], SC[0:1, 0:1], 0.0, None, ALU.is_gt).then_inc(gen_ready, 1)

            for m in range(KT):
                layer1(0, m)
            turn(0, 0, 0, True, None, None)
            turn(0, 1, 1, True, None, 0)
            with dve.Fori(2, CHUNKS - 1) as k:
                turn(0, k, k, True, None, k - 1)
            late_turn(0, CHUNKS - 1, CHUNKS - 1, CHUNKS - 2, 0)

            def round_(r):
                gb = r * CHUNKS
                if isinstance(r, int):
                    late_turn(1, 0, CHUNKS, CHUNKS - 1, 1)
                else:
                    restart(r)
                    attention(gb, 0)
                    stats("f", gb + CHUNKS, FR, st_f, mv_f)
                    normalise("f", gb + CHUNKS, FR, mv_f, rs_f, xnt_f)
                    xn_low(gb + CHUNKS)
                    attention(gb + 1, 1)
                    for m in range(KT):
                        layer1(gb + CHUNKS, m)
                    turn(1, 0, gb + CHUNKS, True, (gb + 2, 2), None)
                with dve.Fori(1, CHUNKS - 2) as k:
                    turn(1, k, gb + k + CHUNKS, True, (gb + k + 2, k + 2), None)
                if isinstance(r, int):
                    dve.wait_ge(step_h, (FIRST_PASS + CHUNKS) * CSTEPS)
                    nc.vector.tensor_tensor(h_ne[:, 1:BLOCKS], h_all[:, 1:BLOCKS],
                                            h_all[:, STEPS * BLOCKS:STEPS * BLOCKS + BLOCKS - 1],
                                            ALU.not_equal).then_inc(h_ne_r, 1)
                    dve.wait_ge(h_ne_r, 1)
                    nc.vector.reduce_sum(h_nes[:, :], h_ne[:, 1:BLOCKS], axis=mybir.AxisListType.X).then_inc(h_nes_r, 1)
                turn(1, CHUNKS - 2, gb + 2 * CHUNKS - 2, True, None, None)
                if isinstance(r, int):
                    dve.wait_ge(agree_mm, 1)
                    nc.vector.tensor_scalar(again[:, :], MI[0:1, 0:1], 0.0, None, ALU.is_gt).then_inc(again_r, 1)
                turn(1, CHUNKS - 1, gb + 2 * CHUNKS - 1, False, None, None)

            round_(0)
            dve.wait_ge(again_r, 1)
            need = dve.value_load(again[0:1, 0:1], min_val=0, max_val=1)
            with dve.If(need != 0):
                with dve.Fori(1, ROUNDS) as r:
                    round_(r)

        @block.scalar
        def _(act):
            def front(g):
                act.wait_ge(feat["f"], g + 1)
                wait(act, l1_mm, 4 * g)
                nc.scalar.copy(xn_hi[:, :], FR[:, :]).then_inc(xn_hi_r, 1)

            def layer1(g, m):
                act.wait_ge(l1_mm, 4 * g + m + 1)
                wait(act, u_r, 4 * g + m - 1)
                nc.scalar.activation(th[:, m % 2, :], B1[m][0][:, :], ACT.Tanh, scale=s1h[:, m:m + 1]).then_inc(th_r, 1)

            def gelu(g, m, mm, bankt, s, y_hi, y_read, next_mm, hi_r):
                act.wait_ge(mm, 4 * g + m + 1)
                wait(act, *y_read)
                nc.scalar.activation(y23[:, m, :], bankt[:, :], ACT.Gelu, scale=s)
                wait(act, *next_mm)
                nc.scalar.activation(y_hi[:, m, :], bankt[:, :], ACT.Gelu, scale=s).then_inc(hi_r, 1)

            def gelu2(g, m):
                gelu(g, m, l2_mm, B2[m], sc[:, 2 * KT + m:2 * KT + m + 1], y2_hi,
                     (y3_lo_pool if m % 2 == 0 else y3_lo_dve, 2 * g + m // 2 - 1), (l3_mm, 4 * g), y2_hi_r)

            def gelu3(g, m):
                gelu(g, m, l3_mm, B3[m], sc[:, 3 * KT + m:3 * KT + m + 1], y3_hi,
                     (y2_lo_pool if m % 2 == 0 else y2_lo_dve, 2 * g + m // 2 + 1), (l4_mm, g), y3_hi_r)

            def middle_copy(c):
                act.wait_ge(feat["m"], c + 1)
                nc.scalar.copy(xn2[:, :], MI[:, :]).then_inc(xn2_r, 1)

            def xb_copy(c):
                act.wait_ge(xb_mm, c + 1)
                nc.scalar.copy(cols(xb_all, (c + FIRST) % CHUNKS if isinstance(c, int) else c + FIRST, HCOLS), MI[:, 0:HCOLS]).then_inc(xb_r, 1)

            def scan_step(n, c, t):
                act.wait_ge(step_mm, n * CSTEPS + t + 1)
                nc.scalar.activation(h_all[:, bass.ds(c * HCOLS + (t + 1) * BLOCKS, BLOCKS)],
                                     SC[:, t * BLOCKS:(t + 1) * BLOCKS], ACT.Tanh).then_inc(step_h, 1)

            def turn(g, nxt, scan, mid):
                def step(t):
                    if scan is not None:
                        scan_step(scan[0], scan[1], t)
                gelu2(g, 0)
                step(0)
                gelu2(g, 1)
                step(1)
                if nxt:
                    front(g + 1)
                gelu2(g, 2)
                step(2)
                if mid is not None:
                    middle_copy(mid)
                gelu2(g, 3)
                step(3)
                if nxt:
                    layer1(g + 1, 0)
                    layer1(g + 1, 1)
                step(4)
                gelu3(g, 0)
                step(5)
                if nxt:
                    layer1(g + 1, 2)
                gelu3(g, 1)
                step(6)
                if nxt:
                    layer1(g + 1, 3)
                gelu3(g, 2)
                step(7)
                gelu3(g, 3)
                if mid is not None:
                    xb_copy(mid)

            def late_turn(g, mid, c):
                def steps(n, cc, ts):
                    for t in ts:
                        scan_step(n, cc, t)
                if c == 0:
                    steps(FIRST_PASS - 1, CHUNKS - 1, range(KT))
                gelu2(g, 0)
                if c == 0:
                    steps(FIRST_PASS - 1, CHUNKS - 1, range(KT, CSTEPS))
                gelu2(g, 1)
                middle_copy(mid)
                gelu2(g, 2)
                xb_copy(mid)
                steps(FIRST_PASS + c, c, range(KT))
                gelu2(g, 3)
                steps(FIRST_PASS + c, c, range(KT, CSTEPS))
                gelu3(g, 0)
                gelu3(g, 1)
                gelu3(g, 2)
                front(g + 1)
                gelu3(g, 3)
                for m in range(KT):
                    layer1(g + 1, m)
                    if c == 1:
                        steps(FIRST_PASS + 2, 2, (2 * m, 2 * m + 1))

            def hi_part(i):
                off, width = PIECES[i]
                act.wait_ge(ld_w[i], 16)
                nc.scalar.copy(w_hi[:, off:off + width], w_raw[:, off:off + width]).then_inc(w_hi_ready, 1)

            for i in range(2):
                hi_part(i)
            act.wait_ge(cw_mm, 1)
            act.wait_ge(ld_c, 48)
            for b in range(SEQS):
                i = nc.scalar.activation(cw_pad[:, b, :], MI[:, 0:P], ACT.Copy, scale=mask[:, b:b + 1])
            i.then_inc(cw_ready, 1)
            hi_part(2)
            front(0)
            for i in range(3, len(PIECES)):
                hi_part(i)
            act.wait_ge(ld_sc, 16)
            act.wait_ge(set_up, 4)
            for m in range(KT):
                layer1(0, m)
            turn(0, True, None, None)
            turn(1, True, None, 0)
            with act.Fori(2, CHUNKS - 1) as k:
                turn(k, True, (k - 2, k - 2 + FIRST), k - 1)
            late_turn(CHUNKS - 1, CHUNKS - 2, 0)

            def round_(r):
                gb = r * CHUNKS
                n = gb + FIRST_PASS
                if isinstance(r, int):
                    late_turn(CHUNKS, CHUNKS - 1, 1)
                else:
                    for t in range(CSTEPS):
                        scan_step(n, 0, t)
                    for t in range(CSTEPS):
                        scan_step(n + 1, 1, t)
                    front(gb + CHUNKS)
                    for m in range(KT):
                        layer1(gb + CHUNKS, m)
                    turn(gb + CHUNKS, True, (n + 2, 2), None)
                with act.Fori(1, CHUNKS - 2) as k:
                    turn(gb + k + CHUNKS, True, (n + k + 2, k + 2), None)
                turn(gb + 2 * CHUNKS - 2, True, None, None)
                turn(gb + 2 * CHUNKS - 1, False, None, None)

            round_(0)
            act.wait_ge(again_r, 1)
            need = act.value_load(again[0:1, 0:1], min_val=0, max_val=1)
            with act.If(need != 0):
                with act.Fori(1, ROUNDS) as r:
                    round_(r)

        @block.gpsimd
        def _(pool):
            def inverse_std(kind, g, mv, ve, rs):
                pool.wait_ge(var[kind], g + 1)
                pool.tensor_tensor(ve[:, :], mv[:, :, 1], epsc[:, :], ALU.add).then_inc(veps[kind], 1)
                pool.wait_ge(veps[kind], g + 1)
                wait(pool, normed[kind], g)
                pool.tensor_tensor(rs[:, :], ve[:, :], mhalf[:, :], ALU.pow).then_inc(rstd[kind], 1)

            def low(g, k, hi_r, per, y, y_hi, y_lo, out_sem, free):
                pool.wait_ge(hi_r, 4 * g + k + 1)
                wait(pool, *free)
                pool.tensor_tensor(y_lo[:, k, :], y[:, k, :], y_hi[:, k, :].bitcast(F32), ALU.subtract).then_inc(out_sem, 1)

            def layer1(g):
                for m in range(KT):
                    low(g, m, y1_hi_r, 4, y1, y1_hi, y1_lo, y1_lo_r, (l2_mm, 4 * g))

            def turn(g, nxt, mid):
                if nxt:
                    inverse_std("f", g + 1, mv_f, ve_f, rs_f)
                if mid is not None:
                    inverse_std("m", mid, mv_m, ve_m, rs_m)
                low(g, 0, y2_hi_r, 2, y23, y2_hi, y2_lo, y2_lo_pool, (l3_mm, 4 * g))
                low(g, 2, y2_hi_r, 2, y23, y2_hi, y2_lo, y2_lo_pool, (l3_mm, 4 * g))
                if nxt:
                    layer1(g + 1)
                low(g, 0, y3_hi_r, 2, y23, y3_hi, y3_lo, y3_lo_pool, (l4_mm, g))
                low(g, 2, y3_hi_r, 2, y23, y3_hi, y3_lo, y3_lo_pool, (l4_mm, g))

            def late_turn(g, mid):
                inverse_std("m", mid, mv_m, ve_m, rs_m)
                low(g, 0, y2_hi_r, 2, y23, y2_hi, y2_lo, y2_lo_pool, (l3_mm, 4 * g))
                low(g, 2, y2_hi_r, 2, y23, y2_hi, y2_lo, y2_lo_pool, (l3_mm, 4 * g))
                inverse_std("f", g + 1, mv_f, ve_f, rs_f)
                low(g, 0, y3_hi_r, 2, y23, y3_hi, y3_lo, y3_lo_pool, (l4_mm, g))
                low(g, 2, y3_hi_r, 2, y23, y3_hi, y3_lo, y3_lo_pool, (l4_mm, g))
                layer1(g + 1)

            pool.memset(a_blk[:, :], 0.0).then_inc(pool_set, 1)
            pool.wait_ge(set_up, 1)
            pool.wait_ge(ld_w[0], 16)
            pool.wait_ge(ld_w[1], 16)
            pool.wait_ge(w_hi_ready, 2)
            pool.tensor_tensor(w_lo[:, 0:WOFF[2]], w_raw[:, 0:WOFF[2]], w_hi[:, 0:WOFF[2]].bitcast(F32),
                               ALU.subtract).then_inc(w_lo1_ready, 1)
            inverse_std("f", 0, mv_f, ve_f, rs_f)
            pool.memset(b_pad[:, :, :], 0.0).then_inc(pool_set, 1)
            pool.wait_ge(pool_set, 2)
            pool.wait_ge(ld_c, 48)
            for b in range(SEQS):
                i = pool.tensor_copy(b_pad[:, b, b * STATES:(b + 1) * STATES], b_sb[:, :])
            i.then_inc(pool_set, 1)
            pool.wait_ge(gen_ready, 1)
            is_general = pool.value_load(general[0:1, 0:1], min_val=0, max_val=1)
            with pool.If(is_general != 0):
                pool.tensor_tensor(w_lo[:, WOFF[2]:], w_raw[:, WOFF[2]:], w_hi[:, WOFF[2]:].bitcast(F32),
                                   ALU.subtract).then_inc(w_lo_ready, 1)
            layer1(0)
            turn(0, True, None)
            turn(1, True, 0)
            with pool.Fori(2, CHUNKS - 1) as k:
                turn(k, True, k - 1)
            late_turn(CHUNKS - 1, CHUNKS - 2)

            def round_(r):
                gb = r * CHUNKS
                if isinstance(r, int):
                    late_turn(CHUNKS, CHUNKS - 1)
                else:
                    inverse_std("f", gb + CHUNKS, mv_f, ve_f, rs_f)
                    layer1(gb + CHUNKS)
                    turn(gb + CHUNKS, True, None)
                with pool.Fori(1, CHUNKS - 2) as k:
                    turn(gb + k + CHUNKS, True, None)
                turn(gb + 2 * CHUNKS - 2, True, None)
                turn(gb + 2 * CHUNKS - 1, False, None)

            round_(0)
            pool.wait_ge(again_r, 1)
            need = pool.value_load(again[0:1, 0:1], min_val=0, max_val=1)
            with pool.If(need != 0):
                with pool.Fori(1, ROUNDS) as r:
                    round_(r)

        @block.sync
        def _(sp):
            sp.dma_start(lnin[:, :], xT[:, 0:N]).then_inc(ld_x, 16)
            sp.dma_start(ident[:, :], ident_d).then_inc(ld_c, 16)
            for i, w in enumerate((w1T, w2T)):
                sp.dma_start(w_raw[:, WOFF[i]:WOFF[i + 1]], w).then_inc(ld_w[i], 16)
            sp.dma_start(mask[:, :], mask_d).then_inc(ld_c, 16)
            sp.dma_start(b_sb[:, :], Bm).then_inc(ld_c, 16)
            sp.dma_start(ct[:, :], CTrep).then_inc(ld_a, 16)
            sp.dma_start(wout[:, :], WoutT).then_inc(ld_a, 16)
            sp.dma_start(sc[:, :], scales).then_inc(ld_sc, 16)
            for i, (w, lo, hi) in enumerate(((h1T, 0, HALF), (h1T, HALF, 2 * HALF), (h2T, 0, HALF), (h2T, HALF, 2 * HALF),
                                             (w3T, 0, KT * P)), 2):
                off, width = PIECES[i]
                sp.dma_start(w_raw[:, off:off + width], w[:, lo:hi]).then_inc(ld_w[i], 16)
            sp.wait_ge(tok["f"], 1)
            sp.dma_start(lnin[:, :], xT[:, N:2 * N]).then_inc(ld_x, 16)
            sp.wait_ge(pool_set, 1)
            sp.dma_start(x_all[:, :], xT).then_inc(ld_xall, 16)
            for b in range(SEQS):
                rows = slice(b * STATES, (b + 1) * STATES)
                sp.dma_start(a_blk[rows, rows], AT).then_inc(ld_ab, 16)
            with sp.Fori(0, CHUNKS - 2) as k:
                sp.wait_ge(tok["f"], k + 2)
                sp.dma_start(lnin[:, :], xT[:, bass.ds(k * N + 2 * N, N)]).then_inc(ld_x, 16)
                sp.wait_ge(l4_out, k + 1)
                sp.dma_start(cols(x_all, k), x1c[:, :]).then_inc(x1_saved, 16)
            def save_x1(k):
                sp.wait_ge(l4_out, k + 1)
                sp.dma_start(cols(x_all, k), x1c[:, :]).then_inc(x1_saved, 16)

            save_x1(CHUNKS - 2)

            def round_(r):
                gb = r * CHUNKS
                for c in range(2):
                    sp.wait_ge(x2_r, gb + c + 1)
                    sp.dma_start(cols(x2_all, c), lnin[:, :]).then_inc(x2_saved, 16)
                    if isinstance(r, int) and c == 0:
                        save_x1(CHUNKS - 1)
                with sp.Fori(0, CHUNKS - 2) as k:
                    sp.wait_ge(x2_r, gb + k + 3)
                    sp.dma_start(cols(x2_all, k + 2), lnin[:, :]).then_inc(x2_saved, 16)
                    sp.wait_ge(l4_out, gb + k + CHUNKS + 1)
                    sp.dma_start(outT[:, bass.ds(k * N, N)], outb[:, :]).then_inc(out_sem, 16)
                for k in (CHUNKS - 2, CHUNKS - 1):
                    sp.wait_ge(l4_out, gb + k + CHUNKS + 1)
                    sp.dma_start(outT[:, k * N:(k + 1) * N], outb[:, :]).then_inc(out_sem, 16)

            round_(0)
            sp.wait_ge(again_r, 1)
            need = sp.value_load(again[0:1, 0:1], min_val=0, max_val=1)
            with sp.If(need != 0):
                with sp.Fori(1, ROUNDS) as r:
                    round_(r)
                sp.wait_ge(out_sem, 16 * CHUNKS * ROUNDS)
            with sp.If(need == 0):
                sp.wait_ge(out_sem, 16 * CHUNKS)

def kernel(**inputs):
    import numpy as np
    import concourse.bacc as _bacc
    from concourse import mybir as _mybir
    from concourse.bass_utils import run_bass_kernel_spmd as _run

    v = {k[3:]: np.asarray(a) for k, a in inputs.items()}
    tiles = lambda w: np.ascontiguousarray(w.T.reshape(-1, P, w.shape[0]).transpose(1, 0, 2)).reshape(P, -1)
    col = lambda s: s.reshape(-1, P).T
    arrays = {
        "xT": np.ascontiguousarray(np.roll(v["attn_x"].reshape(SEQS, BLOCKS, CHUNKS, CSTEPS, P), -FIRST, axis=2)
                                   .transpose(4, 2, 0, 3, 1)).reshape(P, -1),
        "w1T": tiles(v["ffn_w1_w"]), "w2T": tiles(v["ffn_w2_w"]), "h1T": tiles(v["ffn_h1_w"]),
        "h2T": tiles(v["ffn_h2_w"]), "w3T": tiles(v["ffn_w3_w"]),
        "scales": np.ascontiguousarray(np.concatenate(
            [col(v[n]) for n in ("ffn_w1_s", "ffn_w2_s", "ffn_h1_s", "ffn_h2_s", "ffn_w3_s", "attn_b_out")], axis=1)),
        "AT": np.ascontiguousarray(v["attn_A"].T),
        "Bm": np.ascontiguousarray(v["attn_B"]),
        "CTrep": np.ascontiguousarray(np.tile(v["attn_C"].T, (1, SEQS))),
        "WoutT": np.ascontiguousarray(v["attn_W_out"].T),
        "ident": np.eye(P, dtype=np.float32),
        "mask": np.kron(np.eye(SEQS, dtype=np.float32), np.ones((STATES, 1), np.float32)),
    }
    nc = _bacc.Bacc("TRN2", target_bir_lowering=False, num_devices=1)
    args = [nc.dram_tensor(f"in_{n}", a.shape, _mybir.dt.from_np(a.dtype), kind="ExternalInput").ap()
            for n, a in arrays.items()]
    out = nc.dram_tensor("out", (P, CHUNKS * N), F32, kind="ExternalOutput").ap()
    build(nc, *args, out)
    r = _run(nc, [{f"in_{n}": a for n, a in arrays.items()}], core_ids=[0])
    o = np.asarray(r.results[0]["out"]).reshape(P, CHUNKS, SEQS, CSTEPS, BLOCKS)
    return np.ascontiguousarray(o.transpose(2, 4, 1, 3, 0)).reshape(SEQS, LENGTH, P)
```

```python
from contextlib import ExitStack

import concourse.bass as bass
from concourse import mybir

F32 = mybir.dt.float32
F32R = mybir.dt.float32r
I32 = mybir.dt.int32
ALU = mybir.AluOpType
ACT = mybir.ActivationFunctionType

P = 128
SEQS = 8
LENGTH = 512
STATES = 16
BLOCKS = 8
ROUNDS = BLOCKS - 1
STEPS = LENGTH // BLOCKS
CHUNKS = 8
CSTEPS = STEPS // CHUNKS
HCOLS = CSTEPS * BLOCKS
N = SEQS * HCOLS
FIRST = 2
FIRST_PASS = CHUNKS - FIRST
HID = 512
KT = HID // P
QT = N // P
EPS = 1e-5


def wait(engine, sem, value):
    if isinstance(value, int) and value <= 0:
        return
    engine.wait_ge(sem, value)


def build(nc, xT, w1T, w2T, h1T, h2T, w3T, scales, AT, Bm, CTrep, WoutT, ident_d, mask_d, outT):
    with ExitStack() as ctx:
        def sb(name, shape, dt=F32):
            return ctx.enter_context(nc.sbuf_tensor(name, shape, dt))

        def bank(name):
            return ctx.enter_context(nc.psum_tensor(name, [P, N], F32))

        def sem(name):
            return ctx.enter_context(nc.semaphore(name))

        WCOLS = [HID, HID, KT * HID, KT * HID, KT * P]
        WOFF = [sum(WCOLS[:i]) for i in range(6)]
        HALF = KT * HID // 2
        PIECES = [(0, HID), (HID, HID)] + [(WOFF[2] + i * HALF, HALF) for i in range(4)] + [(WOFF[4], KT * P)]
        w_raw = sb("w_raw", [P, WOFF[5]])
        w_hi = sb("w_hi", [P, WOFF[5]], F32R)
        w_lo = sb("w_lo", [P, WOFF[5]], F32R)
        ne_cnt = sb("ne_cnt", [P, len(PIECES)])
        ne_sum = sb("ne_sum", [P, 1])
        sc = sb("sc", [P, 4 * KT + 2])
        s1h = sb("s1h", [P, KT])
        s12h = sb("s12h", [P, KT])
        s3h = sb("s3h", [P, 1])
        ident = sb("ident", [P, P])
        mask = sb("mask", [P, SEQS])
        ones = sb("ones", [P, 1])
        a_blk = sb("a_blk", [P, P])
        b_sb = sb("b_sb", [P, STATES])
        b_rep = sb("b_rep", [P, SEQS, STATES])
        xb_own = sb("xb_own", [P, SEQS, HCOLS])
        ct = sb("ct", [P, P])
        wout = sb("wout", [P, P])
        cw_rep = sb("cw_rep", [P, P])
        x_all = sb("x_all", [P, CHUNKS * N])
        x2_all = sb("x2_all", [P, CHUNKS * N])
        lnin = sb("lnin", [P, N])
        x1c = sb("x1c", [P, N])
        outb = sb("outb", [P, N])
        st_f = sb("st_f", [P, QT, 6])
        st_m = sb("st_m", [P, QT, 6])
        mv_f = sb("mv_f", [P, QT, 2])
        mv_m = sb("mv_m", [P, QT, 2])
        ve_f = sb("ve_f", [P, QT])
        ve_m = sb("ve_m", [P, QT])
        rs_f = sb("rs_f", [P, QT])
        rs_m = sb("rs_m", [P, QT])
        spare = sb("spare", [P, 1])
        mhalf = sb("mhalf", [P, QT])
        epsc = sb("epsc", [P, QT])
        xnt_f = sb("xnt_f", [P, N])
        xnt_m = sb("xnt_m", [P, N])
        xn_hi = sb("xn_hi", [P, N], F32R)
        xn_lo = sb("xn_lo", [P, N], F32R)
        xn2 = sb("xn2", [P, N])
        xb_all = sb("xb_all", [P, CHUNKS * HCOLS])
        h_all = sb("h_all", [P, BLOCKS + STEPS * BLOCKS])
        h_wide = sb("h_wide", [P, SEQS, HCOLS])
        h_ne = sb("h_ne", [P, BLOCKS])
        h_nes = sb("h_nes", [P, 1])
        again = sb("again", [1, 1], I32)
        general = sb("general", [1, 1], I32)
        th = sb("th", [P, 2, N])
        u = sb("u", [P, 2, N])
        y1 = sb("y1", [P, KT, N])
        w_ne = y1[:, :, :].rearrange("p k n -> p (k n)")
        y23 = sb("y23", [P, KT, N])
        y1_hi = sb("y1_hi", [P, KT, N], F32R)
        y1_lo = sb("y1_lo", [P, KT, N], F32R)
        y2_hi = sb("y2_hi", [P, KT, N], F32R)
        y2_lo = sb("y2_lo", [P, KT, N], F32R)
        y3_hi = sb("y3_hi", [P, KT, N], F32R)
        y3_lo = sb("y3_lo", [P, KT, N], F32R)

        F = [bank(f"F{i}") for i in range(5)]
        FR = bank("FR")
        MI = bank("MI")
        SC = bank("SC")
        B2 = [F[0], F[1], F[2], F[3]]
        B1 = [(F[4], F[0]), (F[1], F[2]), (F[4], F[0]), (F[2], F[3])]
        B1_LATE = [(F[4], F[3]), (F[0], FR), (F[1], F[2]), (F[4], F[3])]
        B3 = [F[3], FR, F[4], F[0]]
        B3_LATE = [F[1], F[3], F[4], F[0]]
        B4 = F[1]

        ld_w = [sem(f"ld_w{i}") for i in range(len(PIECES))]
        ld_sc = sem("ld_sc")
        ld_c = sem("ld_c")
        ld_a = sem("ld_a")
        ld_ab = sem("ld_ab")
        ld_x = sem("ld_x")
        ld_xall = sem("ld_xall")
        set_up = sem("set_up")
        pool_set = sem("pool_set")
        w_hi_ready = sem("w_hi_ready")
        w_lo1_ready = sem("w_lo1_ready")
        w_lo_ready = sem("w_lo_ready")
        ne_ready = sem("ne_ready")
        gen_mm = sem("gen_mm")
        gen_ready = sem("gen_ready")
        cw_mm = sem("cw_mm")
        spread = sem("spread")
        cw_ready = sem("cw_ready")
        tok = {k: sem(f"tok_{k}") for k in "fm"}
        bns = {k: sem(f"bns_{k}") for k in "fm"}
        var = {k: sem(f"var_{k}") for k in "fm"}
        veps = {k: sem(f"veps_{k}") for k in "fm"}
        rstd = {k: sem(f"rstd_{k}") for k in "fm"}
        normed = {k: sem(f"normed_{k}") for k in "fm"}
        feat = {k: sem(f"feat_{k}") for k in "fm"}
        xn_hi_r = sem("xn_hi_r")
        xn_lo_r = sem("xn_lo_r")
        l1_mm = sem("l1_mm")
        th_r = sem("th_r")
        u_r = sem("u_r")
        y1_r = sem("y1_r")
        y1_hi_r = sem("y1_hi_r")
        y1_lo_r = sem("y1_lo_r")
        l2_mm = sem("l2_mm")
        y2_hi_r = sem("y2_hi_r")
        y2_lo_dve = sem("y2_lo_dve")
        y2_lo_pool = sem("y2_lo_pool")
        l3_mm = sem("l3_mm")
        y3_hi_r = sem("y3_hi_r")
        y3_lo_dve = sem("y3_lo_dve")
        y3_lo_pool = sem("y3_lo_pool")
        l4_mm = sem("l4_mm")
        l4_out = sem("l4_out")
        x1_saved = sem("x1_saved")
        xn2_r = sem("xn2_r")
        xb_mm = sem("xb_mm")
        xb_own_r = sem("xb_own_r")
        xb_r = sem("xb_r")
        step_mm = sem("step_mm")
        step_h = sem("step_h")
        ends_r = sem("ends_r")
        h_ne_r = sem("h_ne_r")
        h_nes_r = sem("h_nes_r")
        agree_mm = sem("agree_mm")
        again_r = sem("again_r")
        att_mm = sem("att_mm")
        x2_r = sem("x2_r")
        x2_saved = sem("x2_saved")
        out_sem = sem("out_sem")

        block = ctx.enter_context(nc.Block())

        def wtile(w, layer, k, m):
            width = P if layer == 4 else HID
            off = WOFF[layer] + k * width + m * P
            return w[:, off:off + P]

        def cols(t, c, width=N):
            return t[:, bass.ds(c * width, width)]

        def slot(c):
            return (c - FIRST) % CHUNKS if isinstance(c, int) else c - FIRST

        @block.tensor
        def _(pe):
            def split_mm(out, layer, k, m, hi, lo, first, last, gen):
                pairs = [(w_hi, hi), (w_hi, lo)] + ([(w_lo, hi), (w_lo, lo)] if gen else [])
                for i, (w, y) in enumerate(pairs):
                    mm = nc.tensor.matmul(out, wtile(w, layer, k, m), y, start=first and i == 0,
                                          stop=last and i == len(pairs) - 1)
                return mm

            def to_tokens(kind, src, bankt, g, ready, value, att=0):
                pe.wait_ge(ready, value)
                if kind == "f":
                    wait(pe, xn_lo_r, g)
                    wait(pe, y1_r, 4 * g - 2)
                else:
                    wait(pe, xb_r, g)
                    wait(pe, x2_r, att)
                for q in range(QT):
                    mm = nc.tensor.transpose(bankt[:, q * P:(q + 1) * P], src[:, q * P:(q + 1) * P], ident[:, :])
                mm.then_inc(tok[kind], 1)

            def to_features(kind, src, bankt, g):
                pe.wait_ge(normed[kind], g + 1)
                for q in range(QT):
                    mm = nc.tensor.transpose(bankt[:, q * P:(q + 1) * P], src[:, q * P:(q + 1) * P], ident[:, :])
                mm.then_inc(feat[kind], 1)

            def layer1(g, m, gen, late=False):
                if m == 0:
                    pe.wait_ge(xn_lo_r, g + 1)
                if late:
                    if m == 0:
                        wait(pe, y3_hi_r, 4 * g)
                    if m == 2:
                        wait(pe, l4_out, g)
                elif m == 0:
                    wait(pe, y2_hi_r, 4 * g - 3)
                    wait(pe, y3_hi_r, 4 * g - 5)
                elif m == 1:
                    wait(pe, y2_hi_r, 4 * g - 1)
                if m == (3 if late else 2):
                    pe.wait_ge(y1_r, 4 * g + 1)
                if m == 3 and not late:
                    pe.wait_ge(y1_r, 4 * g + 2)
                    wait(pe, y3_hi_r, 4 * g - 3)
                banks = (B1_LATE if late else B1)[m]
                split_mm(banks[0][:, :], 0, 0, m, xn_hi[:, :], xn_lo[:, :], True, True, gen)
                split_mm(banks[1][:, :], 1, 0, m, xn_hi[:, :], xn_lo[:, :], True, True, gen).then_inc(l1_mm, 1)

            def layer2(g, m, gen, beside=lambda k: None):
                if m == 0:
                    wait(pe, y3_hi_r, 4 * g)
                    pe.wait_ge(y1_r, 4 * g + 3)
                if m == 1:
                    wait(pe, l4_out, g)
                for k in range(KT):
                    if m == 0:
                        pe.wait_ge(y1_hi_r, 4 * g + k + 1)
                        pe.wait_ge(y1_lo_r, 4 * g + k + 1)
                    mm = split_mm(B2[m][:, :], 2, k, m, y1_hi[:, k, :], y1_lo[:, k, :], k == 0, k == KT - 1, gen)
                    if k == KT - 1:
                        mm.then_inc(l2_mm, 1)
                    beside(k)

            def layer3(g, m, gen, overlap, banks=B3, beside=lambda k: None):
                if overlap and m >= 2:
                    pe.wait_ge(y1_r, 4 * g + 7)
                for k in range(KT):
                    if m == 0:
                        if banks is B3_LATE:
                            pe.wait_ge(y2_hi_r, 4 * g + max(k, 1) + 1)
                        elif k == 0:
                            pe.wait_ge(y2_hi_r, 4 * g + 4)
                        pe.wait_ge(y2_lo_pool if k % 2 == 0 else y2_lo_dve, 2 * g + k // 2 + 1)
                    if m == 1 and k == 0 and banks is B3_LATE:
                        pe.wait_ge(y2_hi_r, 4 * g + 4)
                    mm = split_mm(banks[m][:, :], 3, k, m, y2_hi[:, k, :], y2_lo[:, k, :], k == 0, k == KT - 1, gen)
                    if k == KT - 1:
                        mm.then_inc(l3_mm, 1)
                    beside(k)

            def layer4(g, gen):
                for k in range(KT):
                    pe.wait_ge(y3_hi_r, 4 * g + k + 1)
                    if k == 0:
                        pe.wait_ge(y3_lo_pool, g + 1)
                    else:
                        pe.wait_ge(y3_lo_dve, (KT - 1) * g + k)
                    mm = split_mm(B4[:, :], 4, k, 0, y3_hi[:, k, :], y3_lo[:, k, :], k == 0, k == KT - 1, gen)
                mm.then_inc(l4_mm, 1)

            def x_times_b(c):
                pe.wait_ge(xn2_r, c + 1)
                mm = nc.tensor.matmul(MI[:, :], b_rep[:, :, :].rearrange("p b n -> p (b n)"), xn2[:, :],
                                      start=True, stop=True)
                mm.then_inc(xb_mm, 1)

            def scan_step(n, c, t, xb_chunks=None):
                s = n * CSTEPS + t
                if t == 0:
                    if xb_chunks is not None:
                        pe.wait_ge(xb_r, xb_chunks)
                    wait(pe, step_h, s)
                    nc.tensor.matmul(SC[:, 0:HCOLS], ident[:, :], cols(xb_all, c, HCOLS), start=True, stop=False,
                                     skip_group_check=True)
                wait(pe, step_h, s)
                off = c * HCOLS + t * BLOCKS
                nc.tensor.matmul(SC[:, t * BLOCKS:(t + 1) * BLOCKS], a_blk[:, :], h_all[:, bass.ds(off, BLOCKS)],
                                 start=False, stop=t == CSTEPS - 1, skip_group_check=True).then_inc(step_mm, 1)

            def attention(gb, c):
                pe.wait_ge(spread, gb + 1)
                wait(pe, x2_r, gb)
                mm = nc.tensor.matmul(MI[:, :], cw_rep[:, :], h_wide[:, :, :].rearrange("p b s -> p (b s)"),
                                      start=True, stop=True)
                mm.then_inc(att_mm, 1)

            def turn(phase, k, g, gen, nxt, scan, mid):
                def step(t):
                    if scan is not None:
                        scan_step(scan[0], scan[1], t, scan[0] + 1 if phase == 0 else None)
                if nxt:
                    if phase == 0:
                        to_tokens("f", lnin, FR, g + 1, ld_x, 16 * (k + 2))
                    else:
                        to_tokens("f", lnin, FR, g + 1, x2_r, g + 2 - CHUNKS)
                layer2(g, 0, gen)
                step(0)
                if mid is not None:
                    to_tokens("m", x1c, MI, mid, l4_out, mid + 1)
                layer2(g, 1, gen)
                step(1)
                layer2(g, 2, gen)
                step(2)
                if nxt:
                    to_features("f", xnt_f, FR, g + 1)
                layer2(g, 3, gen)
                if mid is not None:
                    to_features("m", xnt_m, MI, mid)
                if mid is not None:
                    step(3)
                if nxt:
                    layer1(g + 1, 0, gen)
                if mid is None:
                    step(3)
                if nxt:
                    layer1(g + 1, 1, gen)
                step(4)
                layer3(g, 0, gen, nxt)
                step(5)
                if nxt:
                    layer1(g + 1, 2, gen)
                layer3(g, 1, gen, nxt)
                step(6)
                if nxt:
                    layer1(g + 1, 3, gen)
                layer3(g, 2, gen, nxt)
                step(7)
                layer3(g, 3, gen, nxt)
                if mid is not None:
                    if isinstance(mid, int) and mid == 0:
                        pe.wait_ge(pool_set, 2)
                        pe.wait_ge(ld_ab, 16 * SEQS)
                    x_times_b(mid)
                if phase == 1 and scan is not None:
                    attention(scan[0] - FIRST_PASS, scan[1])
                layer4(g, gen)

            def late_turn(g, gen, mid, c):
                to_tokens("m", x1c, MI, mid, l4_out, mid + 1, att=c)
                for m in range(2):
                    def step(k):
                        if c == 0:
                            scan_step(FIRST_PASS - 1, CHUNKS - 1, KT * m + k, FIRST_PASS)
                    layer2(g, m, gen, step)
                to_features("m", xnt_m, MI, mid)
                layer2(g, 2, gen)
                x_times_b(mid)
                if c == 0:
                    pe.wait_ge(ends_r, 1)
                    pe.wait_ge(cw_ready, 1)
                layer2(g, 3, gen, lambda k: scan_step(FIRST_PASS + c, c, k, mid + 1))
                layer3(g, 0, gen, False, B3_LATE, lambda k: scan_step(FIRST_PASS + c, c, KT + k))
                layer3(g, 1, gen, False, B3_LATE, lambda k: attention(c, c) if k == 1 else None)
                to_tokens("f", lnin, FR, g + 1, x2_r, c + 1)
                layer3(g, 2, gen, False, B3_LATE)
                layer3(g, 3, gen, False, B3_LATE)
                to_features("f", xnt_f, FR, g + 1)
                layer4(g, gen)
                for m in range(KT):
                    layer1(g + 1, m, gen, late=True)
                    if c == 1:
                        for t in (2 * m, 2 * m + 1):
                            scan_step(FIRST_PASS + 2, 2, t)
                if c == 1:
                    attention(2, 2)

            def program(gen):
                pe.wait_ge(w_hi_ready, len(PIECES))
                for m in range(2, KT):
                    layer1(0, m, gen, late=True)
                if gen:
                    pe.wait_ge(w_lo_ready, 1)
                turn(0, 0, 0, gen, True, None, None)
                turn(0, 1, 1, gen, True, None, 0)
                turn(0, 2, 2, gen, True, (0, FIRST), 1)
                with pe.Fori(3, CHUNKS - 1) as k:
                    turn(0, k, k, gen, True, (k - 2, k - 2 + FIRST), k - 1)
                late_turn(CHUNKS - 1, gen, CHUNKS - 2, 0)

                def round_(r):
                    gb = r * CHUNKS
                    n = gb + FIRST_PASS
                    if isinstance(r, int):
                        late_turn(CHUNKS, gen, CHUNKS - 1, 1)
                    else:
                        pe.wait_ge(ends_r, r + 1)
                        for t in range(CSTEPS):
                            scan_step(n, 0, t)
                        attention(gb, 0)
                        to_tokens("f", lnin, FR, gb + CHUNKS, x2_r, gb + 1)
                        for t in range(CSTEPS):
                            scan_step(n + 1, 1, t)
                        to_features("f", xnt_f, FR, gb + CHUNKS)
                        attention(gb + 1, 1)
                        for m in range(KT):
                            layer1(gb + CHUNKS, m, gen, late=True)
                        turn(1, 0, gb + CHUNKS, gen, True, (n + 2, 2), None)
                    with pe.Fori(1, CHUNKS - 2) as k:
                        turn(1, k, gb + k + CHUNKS, gen, True, (n + k + 2, k + 2), None)
                    turn(1, CHUNKS - 2, gb + 2 * CHUNKS - 2, gen, True, None, None)
                    if isinstance(r, int):
                        pe.wait_ge(h_nes_r, 1)
                        nc.tensor.matmul(MI[0:1, 0:1], h_nes[:, :], ones[:, :], start=True, stop=True).then_inc(agree_mm, 1)
                    turn(1, CHUNKS - 1, gb + 2 * CHUNKS - 1, gen, False, None, None)

                round_(0)
                pe.wait_ge(again_r, 1)
                need = pe.value_load(again[0:1, 0:1], min_val=0, max_val=1)
                with pe.If(need != 0):
                    with pe.Fori(1, ROUNDS) as r:
                        round_(r)

            pe.wait_ge(ld_c, 48)
            to_tokens("f", lnin, FR, 0, ld_x, 16)
            pe.wait_ge(ld_a, 32)
            nc.tensor.matmul(MI[:, 0:P], ct[:, :], wout[:, :], start=True, stop=True).then_inc(cw_mm, 1)
            to_features("f", xnt_f, FR, 0)
            pe.wait_ge(w_hi_ready, 2)
            pe.wait_ge(w_lo1_ready, 1)
            layer1(0, 0, True, late=True)
            pe.wait_ge(ne_ready, len(PIECES) + 1)
            pe.wait_ge(set_up, 1)
            nc.tensor.matmul(SC[0:1, 0:1], ne_sum[:, :], ones[:, :], start=True, stop=True).then_inc(gen_mm, 1)
            layer1(0, 1, True, late=True)
            pe.wait_ge(gen_ready, 1)
            is_general = pe.value_load(general[0:1, 0:1], min_val=0, max_val=1)
            with pe.If(is_general == 0):
                program(False)
            with pe.If(is_general != 0):
                program(True)

        @block.vector
        def _(dve):
            def stats(kind, g, bankt, st, mv):
                dve.wait_ge(tok[kind], g + 1)
                for q in range(QT):
                    i = nc.vector.bn_stats(st[:, q, :], bankt[:, q * P:(q + 1) * P])
                i.then_inc(bns[kind], 1)
                dve.wait_ge(bns[kind], g + 1)
                nc.vector.memset(spare[:, :], 0.0)
                for q in range(QT):
                    i = nc.vector.bn_aggr(mv[:, q, :], st[:, q, :])
                i.then_inc(var[kind], 1)

            def normalise(kind, g, bankt, mv, rs, out):
                dve.wait_ge(rstd[kind], g + 1)
                wait(dve, feat[kind], g)
                for q in range(QT):
                    i = nc.vector.tensor_scalar(out[:, q * P:(q + 1) * P], bankt[:, q * P:(q + 1) * P],
                                                mv[:, q, 0:1], rs[:, q:q + 1], ALU.subtract, ALU.mult)
                i.then_inc(normed[kind], 1)

            def xn_low(g):
                dve.wait_ge(xn_hi_r, g + 1)
                nc.vector.tensor_tensor(xn_lo[:, :], FR[:, :], xn_hi[:, :].bitcast(F32), ALU.subtract).then_inc(xn_lo_r, 1)

            def layer1(g, m, late=False):
                banks = (B1_LATE if late else B1)[m]
                dve.wait_ge(th_r, 4 * g + m + 1)
                wait(dve, y1_r, 4 * g + m - 1)
                nc.vector.scalar_tensor_tensor(out=u[:, m % 2, :], in0=th[:, m % 2, :], scalar=1.0, in1=banks[0][:, :],
                                               op0=ALU.add, op1=ALU.mult).then_inc(u_r, 1)
                dve.wait_ge(u_r, 4 * g + m + 1)
                wait(dve, y1_lo_r, 4 * g - 3 + m)
                nc.vector.scalar_tensor_tensor(out=y1[:, m, :], in0=banks[1][:, :], scalar=s12h[:, m:m + 1],
                                               in1=u[:, m % 2, :], op0=ALU.mult, op1=ALU.mult).then_inc(y1_r, 1)
                if late:
                    return
                dve.wait_ge(y1_r, 4 * g + m + 1)
                wait(dve, l2_mm, 4 * g)
                nc.vector.tensor_copy(y1_hi[:, m, :], y1[:, m, :]).then_inc(y1_hi_r, 1)

            def low(g, k, hi_r, y, y_hi, y_lo, out_sem):
                dve.wait_ge(hi_r, 4 * g + k + 1)
                nc.vector.tensor_tensor(y_lo[:, k, :], y[:, k, :], y_hi[:, k, :].bitcast(F32), ALU.subtract).then_inc(out_sem, 1)

            def layer4(phase, g, c):
                dve.wait_ge(l4_mm, g + 1)
                if phase == 0:
                    dve.wait_ge(ld_xall, 16)
                    wait(dve, x1_saved, 16 * g)
                    wait(dve, tok["m"], g)
                    res, dst = cols(x_all, c), x1c[:, :]
                else:
                    gb = g - CHUNKS
                    dve.wait_ge(x2_saved, 16 * (gb + 1))
                    wait(dve, out_sem, 16 * gb)
                    res, dst = cols(x2_all, c), outb[:, :]
                nc.vector.scalar_tensor_tensor(out=dst, in0=B4[:, :], scalar=s3h[:, :], in1=res,
                                               op0=ALU.mult, op1=ALU.add).then_inc(l4_out, 1)

            def spread_states(gb, c):
                dve.wait_ge(step_h, (gb + FIRST_PASS + 1) * CSTEPS)
                wait(dve, att_mm, gb)
                states = h_all[:, bass.ds(c * HCOLS + BLOCKS, HCOLS)]
                nc.vector.tensor_tensor(h_wide[:, :, :], states.unsqueeze(1).broadcast_to([P, SEQS, HCOLS]),
                                        mask[:, :].unsqueeze(2).broadcast_to([P, SEQS, HCOLS]), ALU.mult).then_inc(spread, 1)

            def attention(gb, c):
                dve.wait_ge(att_mm, gb + 1)
                wait(dve, x2_saved, 16 * gb)
                dve.wait_ge(tok["f"], gb + CHUNKS)
                dve.wait_ge(x1_saved, 16 * min(slot(c) + 1, CHUNKS) if isinstance(c, int) else 16 * CHUNKS)
                nc.vector.scalar_tensor_tensor(out=lnin[:, :], in0=MI[:, :], scalar=sc[:, 4 * KT + 1:4 * KT + 2],
                                               in1=cols(x_all, slot(c)), op0=ALU.add, op1=ALU.add).then_inc(x2_r, 1)

            def own_xb(c):
                dve.wait_ge(xb_mm, c + 1)
                wait(dve, xb_r, c)
                nc.vector.tensor_tensor(xb_own[:, :, :], MI[:, :].rearrange("p (b s) -> p b s", b=SEQS),
                                        mask[:, :].unsqueeze(2).broadcast_to([P, SEQS, HCOLS]), ALU.mult).then_inc(xb_own_r, 1)
                dve.wait_ge(xb_own_r, c + 1)
                place = (c + FIRST) % CHUNKS if isinstance(c, int) else c + FIRST
                nc.vector.reduce_sum(cols(xb_all, place, HCOLS), xb_own[:, :, :].rearrange("p b s -> p s b"),
                                     axis=mybir.AxisListType.X).then_inc(xb_r, 1)

            def restart(r):
                dve.wait_ge(step_h, (r * CHUNKS + FIRST_PASS) * CSTEPS)
                nc.vector.tensor_copy(h_all[:, 1:BLOCKS], h_all[:, STEPS * BLOCKS:STEPS * BLOCKS + BLOCKS - 1]).then_inc(ends_r, 1)

            def late_turn(phase, k, g, mid, c):
                stats("m", mid, MI, st_m, mv_m)
                normalise("m", mid, MI, mv_m, rs_m, xnt_m)
                low(g, 1, y2_hi_r, y23, y2_hi, y2_lo, y2_lo_dve)
                own_xb(mid)
                if c == 0:
                    restart(0)
                low(g, 3, y2_hi_r, y23, y2_hi, y2_lo, y2_lo_dve)
                spread_states(c, c)
                attention(c, c)
                stats("f", g + 1, FR, st_f, mv_f)
                normalise("f", g + 1, FR, mv_f, rs_f, xnt_f)
                low(g, 1, y3_hi_r, y23, y3_hi, y3_lo, y3_lo_dve)
                low(g, 2, y3_hi_r, y23, y3_hi, y3_lo, y3_lo_dve)
                xn_low(g + 1)
                low(g, 3, y3_hi_r, y23, y3_hi, y3_lo, y3_lo_dve)
                layer4(phase, g, k)
                for m in range(KT):
                    layer1(g + 1, m, late=True)
                if c == 1:
                    spread_states(2, 2)
                    attention(2, 2)

            def turn(phase, k, g, nxt, att, mid):
                if nxt:
                    stats("f", g + 1, FR, st_f, mv_f)
                if mid is not None:
                    stats("m", mid, MI, st_m, mv_m)
                if nxt:
                    normalise("f", g + 1, FR, mv_f, rs_f, xnt_f)
                low(g, 1, y2_hi_r, y23, y2_hi, y2_lo, y2_lo_dve)
                if mid is not None:
                    normalise("m", mid, MI, mv_m, rs_m, xnt_m)
                if nxt:
                    xn_low(g + 1)
                low(g, 3, y2_hi_r, y23, y2_hi, y2_lo, y2_lo_dve)
                if nxt:
                    for m in range(KT):
                        layer1(g + 1, m)
                if att is not None:
                    spread_states(att[0], att[1])
                low(g, 1, y3_hi_r, y23, y3_hi, y3_lo, y3_lo_dve)
                low(g, 2, y3_hi_r, y23, y3_hi, y3_lo, y3_lo_dve)
                low(g, 3, y3_hi_r, y23, y3_hi, y3_lo, y3_lo_dve)
                if mid is not None:
                    own_xb(mid)
                if att is not None:
                    attention(att[0], att[1])
                layer4(phase, g, k)

            def count(i):
                off, width = PIECES[i]
                dve.wait_ge(w_hi_ready, i + 1)
                wait(dve, ne_ready, i - 1)
                nc.vector.scalar_tensor_tensor(out=w_ne[:, (i % 2) * HALF:(i % 2) * HALF + width],
                                               in0=w_raw[:, off:off + width], scalar=0.0,
                                               in1=w_hi[:, off:off + width].bitcast(F32), op0=ALU.add,
                                               op1=ALU.not_equal, accum_out=ne_cnt[:, i:i + 1]).then_inc(ne_ready, 1)

            nc.vector.memset(h_all[:, 0:BLOCKS], 0.0)
            nc.vector.memset(h_all[:, FIRST * HCOLS:FIRST * HCOLS + BLOCKS], 0.0)
            nc.vector.memset(ones[:, :], 1.0)
            nc.vector.memset(epsc[:, :], EPS)
            nc.vector.memset(mhalf[:, :], -0.5).then_inc(set_up, 1)
            stats("f", 0, FR, st_f, mv_f)
            count(0)
            normalise("f", 0, FR, mv_f, rs_f, xnt_f)
            count(1)
            dve.wait_ge(ld_sc, 16)
            nc.vector.tensor_scalar(s1h[:, :], sc[:, 0:KT], 0.5, None, ALU.mult).then_inc(set_up, 1)
            nc.vector.tensor_scalar(s3h[:, :], sc[:, 4 * KT:4 * KT + 1], 0.5, None, ALU.mult).then_inc(set_up, 1)
            dve.wait_ge(set_up, 3)
            nc.vector.tensor_tensor(s12h[:, :], s1h[:, :], sc[:, KT:2 * KT], ALU.mult).then_inc(set_up, 1)
            dve.wait_ge(set_up, 4)
            count(2)
            xn_low(0)
            for i in range(3, len(PIECES)):
                count(i)
            dve.wait_ge(ne_ready, len(PIECES))
            nc.vector.reduce_sum(ne_sum[:, :], ne_cnt[:, :], axis=mybir.AxisListType.X).then_inc(ne_ready, 1)
            dve.wait_ge(gen_mm, 1)
            nc.vector.tensor_scalar(general[:, :], SC[0:1, 0:1], 0.0, None, ALU.is_gt).then_inc(gen_ready, 1)

            for m in range(KT):
                layer1(0, m, late=True)
            turn(0, 0, 0, True, None, None)
            turn(0, 1, 1, True, None, 0)
            with dve.Fori(2, CHUNKS - 1) as k:
                turn(0, k, k, True, None, k - 1)
            late_turn(0, CHUNKS - 1, CHUNKS - 1, CHUNKS - 2, 0)

            def round_(r):
                gb = r * CHUNKS
                if isinstance(r, int):
                    late_turn(1, 0, CHUNKS, CHUNKS - 1, 1)
                else:
                    restart(r)
                    spread_states(gb, 0)
                    attention(gb, 0)
                    stats("f", gb + CHUNKS, FR, st_f, mv_f)
                    normalise("f", gb + CHUNKS, FR, mv_f, rs_f, xnt_f)
                    xn_low(gb + CHUNKS)
                    spread_states(gb + 1, 1)
                    attention(gb + 1, 1)
                    for m in range(KT):
                        layer1(gb + CHUNKS, m, late=True)
                    turn(1, 0, gb + CHUNKS, True, (gb + 2, 2), None)
                with dve.Fori(1, CHUNKS - 2) as k:
                    turn(1, k, gb + k + CHUNKS, True, (gb + k + 2, k + 2), None)
                if isinstance(r, int):
                    dve.wait_ge(step_h, (FIRST_PASS + CHUNKS) * CSTEPS)
                    nc.vector.tensor_tensor(h_ne[:, 1:BLOCKS], h_all[:, 1:BLOCKS],
                                            h_all[:, STEPS * BLOCKS:STEPS * BLOCKS + BLOCKS - 1],
                                            ALU.not_equal).then_inc(h_ne_r, 1)
                    dve.wait_ge(h_ne_r, 1)
                    nc.vector.reduce_sum(h_nes[:, :], h_ne[:, 1:BLOCKS], axis=mybir.AxisListType.X).then_inc(h_nes_r, 1)
                turn(1, CHUNKS - 2, gb + 2 * CHUNKS - 2, True, None, None)
                if isinstance(r, int):
                    dve.wait_ge(agree_mm, 1)
                    nc.vector.tensor_scalar(again[:, :], MI[0:1, 0:1], 0.0, None, ALU.is_gt).then_inc(again_r, 1)
                turn(1, CHUNKS - 1, gb + 2 * CHUNKS - 1, False, None, None)

            round_(0)
            dve.wait_ge(again_r, 1)
            need = dve.value_load(again[0:1, 0:1], min_val=0, max_val=1)
            with dve.If(need != 0):
                with dve.Fori(1, ROUNDS) as r:
                    round_(r)

        @block.scalar
        def _(act):
            def front(g):
                act.wait_ge(feat["f"], g + 1)
                wait(act, l1_mm, 4 * g)
                nc.scalar.copy(xn_hi[:, :], FR[:, :]).then_inc(xn_hi_r, 1)

            def layer1(g, m, banks=B1):
                act.wait_ge(l1_mm, 4 * g + m + 1)
                wait(act, u_r, 4 * g + m - 1)
                nc.scalar.activation(th[:, m % 2, :], banks[m][0][:, :], ACT.Tanh, scale=s1h[:, m:m + 1]).then_inc(th_r, 1)

            def y1_high(g, m):
                act.wait_ge(y1_r, 4 * g + m + 1)
                wait(act, l2_mm, 4 * g)
                nc.scalar.copy(y1_hi[:, m, :], y1[:, m, :]).then_inc(y1_hi_r, 1)

            def layer1_late(g, beside=lambda m: None):
                for m in range(KT):
                    layer1(g, m, B1_LATE)
                    beside(m)
                    if m:
                        y1_high(g, m - 1)
                y1_high(g, KT - 1)

            def gelu(g, m, mm, bankt, s, y_hi, y_read, next_mm, hi_r):
                act.wait_ge(mm, 4 * g + m + 1)
                wait(act, *y_read)
                nc.scalar.activation(y23[:, m, :], bankt[:, :], ACT.Gelu, scale=s)
                wait(act, *next_mm)
                nc.scalar.activation(y_hi[:, m, :], bankt[:, :], ACT.Gelu, scale=s).then_inc(hi_r, 1)

            def gelu2(g, m):
                gelu(g, m, l2_mm, B2[m], sc[:, 2 * KT + m:2 * KT + m + 1], y2_hi,
                     (y3_lo_pool, g) if m == 0 else (y3_lo_dve, (KT - 1) * (g - 1) + m), (l3_mm, 4 * g), y2_hi_r)

            def gelu3(g, m, banks=B3):
                gelu(g, m, l3_mm, banks[m], sc[:, 3 * KT + m:3 * KT + m + 1], y3_hi,
                     (y2_lo_pool if m % 2 == 0 else y2_lo_dve, 2 * g + m // 2 + 1), (l4_mm, g), y3_hi_r)

            def middle_copy(c):
                act.wait_ge(feat["m"], c + 1)
                nc.scalar.copy(xn2[:, :], MI[:, :]).then_inc(xn2_r, 1)

            def scan_step(n, c, t):
                act.wait_ge(step_mm, n * CSTEPS + t + 1)
                nc.scalar.activation(h_all[:, bass.ds(c * HCOLS + (t + 1) * BLOCKS, BLOCKS)],
                                     SC[:, t * BLOCKS:(t + 1) * BLOCKS], ACT.Tanh).then_inc(step_h, 1)

            def turn(g, nxt, scan, mid):
                def step(t):
                    if scan is not None:
                        scan_step(scan[0], scan[1], t)
                gelu2(g, 0)
                step(0)
                gelu2(g, 1)
                step(1)
                if nxt:
                    front(g + 1)
                gelu2(g, 2)
                step(2)
                gelu2(g, 3)
                step(3)
                if mid is not None:
                    middle_copy(mid)
                if nxt:
                    layer1(g + 1, 0)
                    layer1(g + 1, 1)
                step(4)
                gelu3(g, 0)
                step(5)
                if nxt:
                    layer1(g + 1, 2)
                gelu3(g, 1)
                step(6)
                if nxt:
                    layer1(g + 1, 3)
                step(7)
                gelu3(g, 2)
                gelu3(g, 3)

            def late_turn(g, mid, c):
                def steps(n, cc, ts):
                    for t in ts:
                        scan_step(n, cc, t)
                if c == 0:
                    steps(FIRST_PASS - 1, CHUNKS - 1, range(KT))
                gelu2(g, 0)
                if c == 0:
                    steps(FIRST_PASS - 1, CHUNKS - 1, range(KT, CSTEPS))
                gelu2(g, 1)
                middle_copy(mid)
                gelu2(g, 2)
                steps(FIRST_PASS + c, c, range(KT))
                gelu2(g, 3)
                steps(FIRST_PASS + c, c, range(KT, CSTEPS))
                gelu3(g, 0, B3_LATE)
                gelu3(g, 1, B3_LATE)
                gelu3(g, 2, B3_LATE)
                gelu3(g, 3, B3_LATE)
                front(g + 1)
                layer1_late(g + 1, lambda m: steps(FIRST_PASS + 2, 2, (2 * m, 2 * m + 1)) if c == 1 else None)

            def hi_part(i):
                off, width = PIECES[i]
                act.wait_ge(ld_w[i], 16)
                nc.scalar.copy(w_hi[:, off:off + width], w_raw[:, off:off + width]).then_inc(w_hi_ready, 1)

            for i in range(2):
                hi_part(i)
            act.wait_ge(cw_mm, 1)
            nc.scalar.copy(cw_rep[:, :], MI[:, 0:P]).then_inc(cw_ready, 1)
            hi_part(2)
            front(0)
            for i in range(3, len(PIECES)):
                hi_part(i)
            act.wait_ge(ld_sc, 16)
            act.wait_ge(set_up, 4)
            layer1_late(0)
            turn(0, True, None, None)
            turn(1, True, None, 0)
            with act.Fori(2, CHUNKS - 1) as k:
                turn(k, True, (k - 2, k - 2 + FIRST), k - 1)
            late_turn(CHUNKS - 1, CHUNKS - 2, 0)

            def round_(r):
                gb = r * CHUNKS
                n = gb + FIRST_PASS
                if isinstance(r, int):
                    late_turn(CHUNKS, CHUNKS - 1, 1)
                else:
                    for t in range(CSTEPS):
                        scan_step(n, 0, t)
                    for t in range(CSTEPS):
                        scan_step(n + 1, 1, t)
                    front(gb + CHUNKS)
                    layer1_late(gb + CHUNKS)
                    turn(gb + CHUNKS, True, (n + 2, 2), None)
                with act.Fori(1, CHUNKS - 2) as k:
                    turn(gb + k + CHUNKS, True, (n + k + 2, k + 2), None)
                turn(gb + 2 * CHUNKS - 2, True, None, None)
                turn(gb + 2 * CHUNKS - 1, False, None, None)

            round_(0)
            act.wait_ge(again_r, 1)
            need = act.value_load(again[0:1, 0:1], min_val=0, max_val=1)
            with act.If(need != 0):
                with act.Fori(1, ROUNDS) as r:
                    round_(r)

        @block.gpsimd
        def _(pool):
            def inverse_std(kind, g, mv, ve, rs):
                pool.wait_ge(var[kind], g + 1)
                pool.tensor_tensor(ve[:, :], mv[:, :, 1], epsc[:, :], ALU.add).then_inc(veps[kind], 1)
                pool.wait_ge(veps[kind], g + 1)
                wait(pool, normed[kind], g)
                pool.tensor_tensor(rs[:, :], ve[:, :], mhalf[:, :], ALU.pow).then_inc(rstd[kind], 1)

            def low(g, k, hi_r, per, y, y_hi, y_lo, out_sem, free):
                pool.wait_ge(hi_r, 4 * g + k + 1)
                wait(pool, *free)
                pool.tensor_tensor(y_lo[:, k, :], y[:, k, :], y_hi[:, k, :].bitcast(F32), ALU.subtract).then_inc(out_sem, 1)

            def layer1(g, ms=range(KT)):
                for m in ms:
                    low(g, m, y1_hi_r, 4, y1, y1_hi, y1_lo, y1_lo_r, (l2_mm, 4 * g))

            def turn(g, nxt, mid):
                if nxt:
                    inverse_std("f", g + 1, mv_f, ve_f, rs_f)
                if mid is not None:
                    inverse_std("m", mid, mv_m, ve_m, rs_m)
                low(g, 0, y2_hi_r, 2, y23, y2_hi, y2_lo, y2_lo_pool, (l3_mm, 4 * g))
                low(g, 2, y2_hi_r, 2, y23, y2_hi, y2_lo, y2_lo_pool, (l3_mm, 4 * g))
                if nxt:
                    layer1(g + 1, range(KT - 1))
                low(g, 0, y3_hi_r, 2, y23, y3_hi, y3_lo, y3_lo_pool, (l4_mm, g))
                if nxt:
                    layer1(g + 1, range(KT - 1, KT))

            def late_turn(g, mid):
                inverse_std("m", mid, mv_m, ve_m, rs_m)
                low(g, 0, y2_hi_r, 2, y23, y2_hi, y2_lo, y2_lo_pool, (l3_mm, 4 * g))
                low(g, 2, y2_hi_r, 2, y23, y2_hi, y2_lo, y2_lo_pool, (l3_mm, 4 * g))
                inverse_std("f", g + 1, mv_f, ve_f, rs_f)
                low(g, 0, y3_hi_r, 2, y23, y3_hi, y3_lo, y3_lo_pool, (l4_mm, g))
                layer1(g + 1)

            pool.memset(a_blk[:, :], 0.0).then_inc(pool_set, 1)
            pool.wait_ge(set_up, 1)
            pool.wait_ge(ld_w[0], 16)
            pool.wait_ge(ld_w[1], 16)
            pool.wait_ge(w_hi_ready, 2)
            pool.tensor_tensor(w_lo[:, 0:WOFF[2]], w_raw[:, 0:WOFF[2]], w_hi[:, 0:WOFF[2]].bitcast(F32),
                               ALU.subtract).then_inc(w_lo1_ready, 1)
            inverse_std("f", 0, mv_f, ve_f, rs_f)
            pool.wait_ge(ld_c, 48)
            for b in range(SEQS):
                i = pool.tensor_copy(b_rep[:, b, :], b_sb[:, :])
            i.then_inc(pool_set, 1)
            pool.wait_ge(gen_ready, 1)
            is_general = pool.value_load(general[0:1, 0:1], min_val=0, max_val=1)
            with pool.If(is_general != 0):
                pool.tensor_tensor(w_lo[:, WOFF[2]:], w_raw[:, WOFF[2]:], w_hi[:, WOFF[2]:].bitcast(F32),
                                   ALU.subtract).then_inc(w_lo_ready, 1)
            layer1(0)
            turn(0, True, None)
            turn(1, True, 0)
            with pool.Fori(2, CHUNKS - 1) as k:
                turn(k, True, k - 1)
            late_turn(CHUNKS - 1, CHUNKS - 2)

            def round_(r):
                gb = r * CHUNKS
                if isinstance(r, int):
                    late_turn(CHUNKS, CHUNKS - 1)
                else:
                    inverse_std("f", gb + CHUNKS, mv_f, ve_f, rs_f)
                    layer1(gb + CHUNKS)
                    turn(gb + CHUNKS, True, None)
                with pool.Fori(1, CHUNKS - 2) as k:
                    turn(gb + k + CHUNKS, True, None)
                turn(gb + 2 * CHUNKS - 2, True, None)
                turn(gb + 2 * CHUNKS - 1, False, None)

            round_(0)
            pool.wait_ge(again_r, 1)
            need = pool.value_load(again[0:1, 0:1], min_val=0, max_val=1)
            with pool.If(need != 0):
                with pool.Fori(1, ROUNDS) as r:
                    round_(r)

        @block.sync
        def _(sp):
            sp.dma_start(lnin[:, :], xT[:, 0:N]).then_inc(ld_x, 16)
            sp.dma_start(ident[:, :], ident_d).then_inc(ld_c, 16)
            for i, w in enumerate((w1T, w2T)):
                sp.dma_start(w_raw[:, WOFF[i]:WOFF[i + 1]], w).then_inc(ld_w[i], 16)
            sp.dma_start(mask[:, :], mask_d).then_inc(ld_c, 16)
            sp.dma_start(b_sb[:, :], Bm).then_inc(ld_c, 16)
            sp.dma_start(ct[:, :], CTrep).then_inc(ld_a, 16)
            sp.dma_start(wout[:, :], WoutT).then_inc(ld_a, 16)
            sp.dma_start(sc[:, :], scales).then_inc(ld_sc, 16)
            for i, (w, lo, hi) in enumerate(((h1T, 0, HALF), (h1T, HALF, 2 * HALF), (h2T, 0, HALF), (h2T, HALF, 2 * HALF),
                                             (w3T, 0, KT * P)), 2):
                off, width = PIECES[i]
                sp.dma_start(w_raw[:, off:off + width], w[:, lo:hi]).then_inc(ld_w[i], 16)
            sp.wait_ge(tok["f"], 1)
            sp.dma_start(lnin[:, :], xT[:, N:2 * N]).then_inc(ld_x, 16)
            sp.wait_ge(pool_set, 1)
            sp.dma_start(x_all[:, :], xT).then_inc(ld_xall, 16)
            for b in range(SEQS):
                rows = slice(b * STATES, (b + 1) * STATES)
                sp.dma_start(a_blk[rows, rows], AT).then_inc(ld_ab, 16)
            with sp.Fori(0, CHUNKS - 2) as k:
                sp.wait_ge(tok["f"], k + 2)
                sp.dma_start(lnin[:, :], xT[:, bass.ds(k * N + 2 * N, N)]).then_inc(ld_x, 16)
                sp.wait_ge(l4_out, k + 1)
                sp.dma_start(cols(x_all, k), x1c[:, :]).then_inc(x1_saved, 16)
            def save_x1(k):
                sp.wait_ge(l4_out, k + 1)
                sp.dma_start(cols(x_all, k), x1c[:, :]).then_inc(x1_saved, 16)

            save_x1(CHUNKS - 2)

            def round_(r):
                gb = r * CHUNKS
                for c in range(2):
                    sp.wait_ge(x2_r, gb + c + 1)
                    sp.dma_start(cols(x2_all, c), lnin[:, :]).then_inc(x2_saved, 16)
                    if isinstance(r, int) and c == 0:
                        save_x1(CHUNKS - 1)
                with sp.Fori(0, CHUNKS - 2) as k:
                    sp.wait_ge(x2_r, gb + k + 3)
                    sp.dma_start(cols(x2_all, k + 2), lnin[:, :]).then_inc(x2_saved, 16)
                    sp.wait_ge(l4_out, gb + k + CHUNKS + 1)
                    sp.dma_start(outT[:, bass.ds(k * N, N)], outb[:, :]).then_inc(out_sem, 16)
                for k in (CHUNKS - 2, CHUNKS - 1):
                    sp.wait_ge(l4_out, gb + k + CHUNKS + 1)
                    sp.dma_start(outT[:, k * N:(k + 1) * N], outb[:, :]).then_inc(out_sem, 16)

            round_(0)
            sp.wait_ge(again_r, 1)
            need = sp.value_load(again[0:1, 0:1], min_val=0, max_val=1)
            with sp.If(need != 0):
                with sp.Fori(1, ROUNDS) as r:
                    round_(r)
                sp.wait_ge(out_sem, 16 * CHUNKS * ROUNDS)
            with sp.If(need == 0):
                sp.wait_ge(out_sem, 16 * CHUNKS)

def kernel(**inputs):
    import numpy as np
    import concourse.bacc as _bacc
    from concourse import mybir as _mybir
    from concourse.bass_utils import run_bass_kernel_spmd as _run

    v = {k[3:]: np.asarray(a) for k, a in inputs.items()}
    tiles = lambda w: np.ascontiguousarray(w.T.reshape(-1, P, w.shape[0]).transpose(1, 0, 2)).reshape(P, -1)
    col = lambda s: s.reshape(-1, P).T
    arrays = {
        "xT": np.ascontiguousarray(np.roll(v["attn_x"].reshape(SEQS, BLOCKS, CHUNKS, CSTEPS, P), -FIRST, axis=2)
                                   .transpose(4, 2, 0, 3, 1)).reshape(P, -1),
        "w1T": tiles(v["ffn_w1_w"]), "w2T": tiles(v["ffn_w2_w"]), "h1T": tiles(v["ffn_h1_w"]),
        "h2T": tiles(v["ffn_h2_w"]), "w3T": tiles(v["ffn_w3_w"]),
        "scales": np.ascontiguousarray(np.concatenate(
            [col(v[n]) for n in ("ffn_w1_s", "ffn_w2_s", "ffn_h1_s", "ffn_h2_s", "ffn_w3_s", "attn_b_out")], axis=1)),
        "AT": np.ascontiguousarray(v["attn_A"].T),
        "Bm": np.ascontiguousarray(v["attn_B"]),
        "CTrep": np.ascontiguousarray(np.tile(v["attn_C"].T, (1, SEQS))),
        "WoutT": np.ascontiguousarray(v["attn_W_out"].T),
        "ident": np.eye(P, dtype=np.float32),
        "mask": np.kron(np.eye(SEQS, dtype=np.float32), np.ones((STATES, 1), np.float32)),
    }
    nc = _bacc.Bacc("TRN2", target_bir_lowering=False, num_devices=1)
    args = [nc.dram_tensor(f"in_{n}", a.shape, _mybir.dt.from_np(a.dtype), kind="ExternalInput").ap()
            for n, a in arrays.items()]
    out = nc.dram_tensor("out", (P, CHUNKS * N), F32, kind="ExternalOutput").ap()
    build(nc, *args, out)
    r = _run(nc, [{f"in_{n}": a for n, a in arrays.items()}], core_ids=[0])
    o = np.asarray(r.results[0]["out"]).reshape(P, CHUNKS, SEQS, CSTEPS, BLOCKS)
    return np.ascontiguousarray(o.transpose(2, 4, 1, 3, 0)).reshape(SEQS, LENGTH, P)
```
